# Optimizing a Trainium2 kernel written in Bass

```python
import numpy as np
import jax
import jax.numpy as jnp

def _softmax(x, axis=-1):
    return jax.nn.softmax(x, axis=axis)

def _gelu(x):
    return jax.nn.gelu(x, approximate=True)

def _silu(x):
    return jax.nn.silu(x)

def _sigmoid(x):
    return jax.nn.sigmoid(x)

def _layernorm(x, axis=-1, eps=1e-05):
    m = jnp.mean(x, axis=axis, keepdims=True)
    v = jnp.var(x, axis=axis, keepdims=True)
    return (x - m) / jnp.sqrt(v + eps)

def _scatter_add(tgt, idx, src, axis=0):
    return tgt.at[idx].add(src)

def _segment_sum(src, seg, n):
    return jax.ops.segment_sum(src, seg, n)
kernel_name = 'mk_vit_tower_d1_tok_img768_r4_8f8e4e'

def setup_inputs(seed: int=0):
    np.random.seed(seed)
    _w = jnp.asarray

    def _rec_inputs():
        import jax
        import jax.numpy as jnp
        _rk = jax.random.key(seed)
        x = -0.000147625 + 0.999875 * jax.random.normal(jax.random.fold_in(_rk, 1), (64, 3, 224, 224), jnp.float32)
        return x
    x = _rec_inputs()

    def _L0_tok_setup():
        import jax, jax.numpy as jnp
        import numpy as np
        N_PATCHES = 14

        def _patchify(images, n_patches):
            n, c, h, w = images.shape
            ps = h // n_patches
            x = images.reshape(n, c, n_patches, ps, n_patches, ps)
            x = x.transpose(0, 2, 4, 1, 3, 5)
            return x.reshape(n, n_patches * n_patches, c * ps * ps)
        key = jax.random.key(seed)
        k1, k2, k3 = jax.random.split(key, 3)
        batch, c, h, w = (64, 3, 224, 224)
        input_dim = c * (h // N_PATCHES) * (w // N_PATCHES)
        hidden_d = 192
        images = jax.random.normal(k1, (batch, c, h, w), dtype=jnp.float32)
        W = jax.random.normal(k2, (hidden_d, input_dim), dtype=jnp.float32) * input_dim ** (-0.5)
        b = jax.random.normal(k3, (hidden_d,), dtype=jnp.float32) * 0.01
        return {'images': images, 'W': W, 'b': b}
    _L0_tok_all = _L0_tok_setup()
    _L0_tok_in = {k: v for k, v in _L0_tok_all.items() if k in ('W', 'b')}
    del _L0_tok_all

    def _L0_attn_setup():
        import jax, jax.numpy as jnp
        import numpy as np
        ALPHA, BETA, GAMMA = (1.9, 3.8, 15.2)
        NUM_HEADS = 12

        def _rp_bucket_euc(height, width, skip):
            coords = np.stack(np.meshgrid(np.arange(height), np.arange(width), indexing='ij'), -1)
            coords = coords.reshape(-1, 2).astype(np.float64)
            diff = coords[:, None, :] - coords[None, :, :]
            dis = np.round(np.sqrt((diff ** 2).sum(-1)))
            log_idx = np.minimum(np.round(ALPHA + np.log(np.maximum(dis, 1e-09) / ALPHA) / np.log(GAMMA / ALPHA) * (BETA - ALPHA)), BETA).astype(np.int64)
            bucket = np.where(dis <= ALPHA, np.round(dis).astype(np.int64), log_idx)
            bucket = bucket - bucket.min()
            nb = 2 * int(BETA) + 1
            if skip > 0:
                L = height * width
                full = np.full((skip + L, skip + L), nb, dtype=np.int64)
                full[skip:, skip:] = bucket
                bucket, nb = (full, nb + 1)
            return (jnp.asarray(bucket), nb)
        key = jax.random.key(seed)
        ks = jax.random.split(key, 4)
        B, N, C = (8, 1025, 192)
        hd = C // NUM_HEADS
        nb = 2 * int(BETA) + 1 + 1
        return {'x': jax.random.normal(ks[0], (B, N, C), jnp.float32), 'qkv_w': jax.random.normal(ks[1], (3 * C, C), jnp.float32) * 0.02, 'proj_w': jax.random.normal(ks[2], (C, C), jnp.float32) * 0.02, 'proj_b': jnp.zeros((C,), jnp.float32), 'rpe_w': jax.random.normal(ks[3], (hd, nb), jnp.float32) * 0.02}
    _L0_attn_all = _L0_attn_setup()
    _L0_attn_in = {k: v for k, v in _L0_attn_all.items() if k in ('qkv_w', 'proj_w', 'proj_b', 'rpe_w')}
    del _L0_attn_all

    def _L0_ffn_setup():
        import jax, jax.numpy as jnp
        import numpy as np
        B, T, C = (4, 512, 192)
        E, K = (8, 2)

        def _mlp(x, wfc, wproj):
            h = jnp.square(jax.nn.relu(x @ wfc))
            return h @ wproj
        key = jax.random.key(seed)
        ks = jax.random.split(key, 6)
        s = 0.02
        return {'x': jax.random.normal(ks[0], (B, T, C), jnp.float32), 'w_fc_sh': jax.random.normal(ks[1], (C, C), jnp.float32) * s, 'w_proj_sh': jax.random.normal(ks[2], (C, C), jnp.float32) * s, 'w1': jax.random.normal(ks[3], (E, C, C), jnp.float32) * s, 'w2': jax.random.normal(ks[4], (E, C, C), jnp.float32) * s, 'router_w': jax.random.normal(ks[5], (E, C), jnp.float32) * s, 'balance_bias': jnp.zeros((E,), jnp.float32)}
    _L0_ffn_all = _L0_ffn_setup()
    _L0_ffn_in = {k: v for k, v in _L0_ffn_all.items() if k in ('w_fc_sh', 'w_proj_sh', 'w1', 'w2', 'router_w', 'balance_bias')}
    del _L0_ffn_all
    return {'x': x, 'L0_tok_W': _L0_tok_in['W'], 'L0_tok_b': _L0_tok_in['b'], 'L0_attn_qkv_w': _L0_attn_in['qkv_w'], 'L0_attn_proj_w': _L0_attn_in['proj_w'], 'L0_attn_proj_b': _L0_attn_in['proj_b'], 'L0_attn_rpe_w': _L0_attn_in['rpe_w'], 'L0_ffn_w_fc_sh': _L0_ffn_in['w_fc_sh'], 'L0_ffn_w_proj_sh': _L0_ffn_in['w_proj_sh'], 'L0_ffn_w1': _L0_ffn_in['w1'], 'L0_ffn_w2': _L0_ffn_in['w2'], 'L0_ffn_router_w': _L0_ffn_in['router_w'], 'L0_ffn_balance_bias': _L0_ffn_in['balance_bias']}

def reference(x, L0_tok_W, L0_tok_b, L0_attn_qkv_w, L0_attn_proj_w, L0_attn_proj_b, L0_attn_rpe_w, L0_ffn_w_fc_sh, L0_ffn_w_proj_sh, L0_ffn_w1, L0_ffn_w2, L0_ffn_router_w, L0_ffn_balance_bias):
    import jax
    import jax.numpy as jnp

    def _L0_tok_ref(images, W, b):
        import jax, jax.numpy as jnp
        import numpy as np
        N_PATCHES = 14

        def _patchify(images, n_patches):
            n, c, h, w = images.shape
            ps = h // n_patches
            x = images.reshape(n, c, n_patches, ps, n_patches, ps)
            x = x.transpose(0, 2, 4, 1, 3, 5)
            return x.reshape(n, n_patches * n_patches, c * ps * ps)
        patches = _patchify(images, N_PATCHES)
        tokens = jnp.einsum('npd,hd->nph', patches, W) + b
        return tokens

    def _L0_attn_ref(x, qkv_w, proj_w, proj_b, rpe_w):
        import jax, jax.numpy as jnp
        import numpy as np
        ALPHA, BETA, GAMMA = (1.9, 3.8, 15.2)
        NUM_HEADS = 12

        def _rp_bucket_euc(height, width, skip):
            coords = np.stack(np.meshgrid(np.arange(height), np.arange(width), indexing='ij'), -1)
            coords = coords.reshape(-1, 2).astype(np.float64)
            diff = coords[:, None, :] - coords[None, :, :]
            dis = np.round(np.sqrt((diff ** 2).sum(-1)))
            log_idx = np.minimum(np.round(ALPHA + np.log(np.maximum(dis, 1e-09) / ALPHA) / np.log(GAMMA / ALPHA) * (BETA - ALPHA)), BETA).astype(np.int64)
            bucket = np.where(dis <= ALPHA, np.round(dis).astype(np.int64), log_idx)
            bucket = bucket - bucket.min()
            nb = 2 * int(BETA) + 1
            if skip > 0:
                L = height * width
                full = np.full((skip + L, skip + L), nb, dtype=np.int64)
                full[skip:, skip:] = bucket
                bucket, nb = (full, nb + 1)
            return (jnp.asarray(bucket), nb)
        B, N, C = x.shape
        H = NUM_HEADS
        hd = C // H
        scale = hd ** (-0.5)
        n_modalities = 1
        height = int((N // n_modalities) ** 0.5)
        skip = N - n_modalities * height * height
        rp_bucket, _ = _rp_bucket_euc(height, height, skip)
        qkv = (x @ qkv_w.T).reshape(B, N, 3, H, hd).transpose(2, 0, 3, 1, 4)
        q, k, v = (qkv[0] * scale, qkv[1], qkv[2])
        attn = jnp.einsum('bhid,bhjd->bhij', q, k)
        lookup = jnp.einsum('bhid,dm->bhim', q, rpe_w)
        bias = jnp.take_along_axis(lookup, rp_bucket[None, None, :, :], axis=3)
        attn = jax.nn.softmax(attn + bias, axis=-1)
        out = jnp.einsum('bhij,bhjd->bhid', attn, v)
        out = out.transpose(0, 2, 1, 3).reshape(B, N, C)
        return out @ proj_w.T + proj_b

    def _L0_ffn_ref(x, w_fc_sh, w_proj_sh, w1, w2, router_w, balance_bias):
        import jax, jax.numpy as jnp
        import numpy as np
        B, T, C = (4, 512, 192)
        E, K = (8, 2)

        def _mlp(x, wfc, wproj):
            h = jnp.square(jax.nn.relu(x @ wfc))
            return h @ wproj
        Bx, Tx, Cx = x.shape
        shared = _mlp(x, w_fc_sh, w_proj_sh)
        xf = x.reshape(-1, Cx)
        logits = xf.astype(jnp.float32) @ router_w.T
        scores = jax.nn.sigmoid(logits)
        _, idx = jax.lax.top_k(scores + balance_bias, K)
        tw = jnp.take_along_axis(scores, idx, axis=-1)
        tw = tw / (tw.sum(-1, keepdims=True) + 1e-20)
        combine = (jax.nn.one_hot(idx, E, dtype=tw.dtype) * tw[..., None]).sum(1)
        h = jnp.square(jax.nn.relu(jnp.einsum('nc,ech->neh', xf, w1)))
        y = jnp.einsum('neh,ehc->nec', h, w2)
        routed = jnp.einsum('nec,ne->nc', y, combine)
        return shared + routed.reshape(Bx, Tx, Cx)
    h = _L0_tok_ref(x, L0_tok_W, L0_tok_b)
    h = h + _L0_attn_ref(_layernorm(h, axis=-1), L0_attn_qkv_w, L0_attn_proj_w, L0_attn_proj_b, L0_attn_rpe_w)
    h = h + _L0_ffn_ref(_layernorm(h, axis=-1), L0_ffn_w_fc_sh, L0_ffn_w_proj_sh, L0_ffn_w1, L0_ffn_w2, L0_ffn_router_w, L0_ffn_balance_bias)
    return h

_drawn_inputs = setup_inputs


def setup_inputs(seed=0):
    import zlib

    import numpy as np

    out = dict(_drawn_inputs(seed))
    spreads = {'L0_attn_proj_b': (0.0, 0.1), 'L0_ffn_balance_bias': (0.0, 0.423)}
    factors = {'L0_tok_b': 5.508,
     'L0_attn_qkv_w': 8.0,
     'L0_attn_proj_w': 8.0,
     'L0_attn_rpe_w': 8.0,
     'L0_ffn_w1': 3.382,
     'L0_ffn_w2': 3.062,
     'L0_ffn_router_w': 4.914,
     'L0_ffn_w_fc_sh': 8.0,
     'L0_ffn_w_proj_sh': 7.805}
    for name, (base, spread) in spreads.items():
        noise = np.random.default_rng([zlib.crc32(name.encode()), seed]).standard_normal(out[name].shape)
        drawn = base * np.exp(spread * noise) if base else spread * noise
        out[name] = jnp.asarray(drawn.astype(out[name].dtype))
    for name, factor in factors.items():
        out[name] = (out[name] * factor).astype(out[name].dtype)
    return out
```

```python
import numpy as np
import concourse.bass as bass
from concourse import mybir
from concourse.alu_op_type import AluOpType as ALU
from contextlib import ExitStack

IMAGES, CHANNELS, SIDE = 64, 3, 224
GRID = 14
PATCH = SIDE // GRID
TOKENS = GRID * GRID
C = 192
HEADS = 12
HD = C // HEADS
EXPERTS = 8
EPS = 1e-5

PAIRS = IMAGES // 2
HALF = TOKENS // 2
TILES = 4
PT = 2 * TOKENS
KX = CHANNELS * PATCH * PATCH // 128
CLO = 128
CHI = C - CLO
SLOT = 32
GROUPS = HEADS // 4
NEAR = 3
VD = C + HEADS * NEAR
HID = (EXPERTS + 1) * C
HT = (HID + 127) // 128
RT = EXPERTS * C // 128
UNITS = 2 * HEADS // 2
OGROUPS = 2 * GROUPS


def buckets():
    alpha, beta, gamma = 1.9, 3.8, 15.2
    at = np.stack(np.meshgrid(np.arange(GRID), np.arange(GRID), indexing="ij"), -1).reshape(-1, 2).astype(np.float64)
    far = np.round(np.sqrt(((at[:, None] - at[None]) ** 2).sum(-1)))
    log = np.minimum(np.round(alpha + np.log(np.maximum(far, 1e-09) / alpha) / np.log(gamma / alpha) * (beta - alpha)), beta)
    b = np.where(far <= alpha, np.round(far).astype(np.int64), log.astype(np.int64))
    return b - b.min()


def window(half, bucket):
    b = buckets()[half * HALF:(half + 1) * HALF]
    cols = np.nonzero((b == bucket).any(0))[0]
    return int(cols.min()), int(cols.max()) + 1


def vit_kernel(nc, a, out):
    f32 = mybir.dt.float32
    u32 = mybir.dt.uint32
    ACT = mybir.ActivationFunctionType
    AX = mybir.AxisListType
    ctx = ExitStack()
    with ctx:
        def sb(name, shape, dt=f32):
            return ctx.enter_context(nc.sbuf_tensor(name, shape, dt))

        def sem(name):
            return ctx.enter_context(nc.semaphore(name))

        w_tok = sb("w_tok", [128, KX, C])
        b_tok = sb("b_tok", [HALF, 2, C])
        w_qk = sb("w_qk", [128, 2, 2 * GROUPS, 128])
        w_qo = sb("w_qo", [128, 2, C])
        rpe_m = sb("rpe_m", [128, 2, HEADS * NEAR])
        rpe_f = sb("rpe_f", [128, 2, HEADS * NEAR])
        rpe_d = sb("rpe_d", [128, 2, HEADS * NEAR])
        k_far = sb("k_far", [128, 1])
        w_vd = sb("w_vd", [128, 2, VD])
        w_proj = sb("w_proj", [128, GROUPS, C])
        b_proj = sb("b_proj", [HALF, TILES, C])
        w_fc = sb("w_fc", [128, 2, HT * 128])
        w_out = sb("w_out", [128, HT, C])
        w_rt = sb("w_rt", [128, 2, EXPERTS])
        b_rt = sb("b_rt", [HALF, TILES, EXPERTS])
        masks = sb("masks", [HALF, 2, NEAR, TOKENS])
        ident = sb("ident", [128, 128])
        rowsum_sel = sb("rowsum_sel", [128, 128])
        expert_sel = sb("expert_sel", [EXPERTS, RT, 128])
        expert_no = sb("expert_no", [HALF, TILES, EXPERTS])
        minus_half = sb("minus_half", [HALF, TILES])
        x = sb("x", [128, KX, PT])
        h = sb("h", [HALF, TILES, C])
        h_pb = sb("h_pb", [HALF, TILES, C])
        stats = sb("stats", [HALF, TILES, 6])
        moments = sb("moments", [HALF, TILES, 2])
        var_eps = sb("var_eps", [HALF, TILES])
        rstd = sb("rstd", [HALF, TILES])
        xn = sb("xn", [HALF, TILES, C])
        xt = sb("xt", [128, 2, PT])
        qk = sb("qk", [128, 2 * GROUPS, PT])
        v = sb("v", [HALF, TILES, HEADS, SLOT])
        diff = sb("diff", [HALF, TILES, HEADS * NEAR])
        neg_max = sb("neg_max", [HALF, 2, 2, 2])
        probs = sb("probs", [HALF, 2, 2, 2, TOKENS])
        probs_t = sb("probs_t", [HALF, 2, 2, 2, TOKENS])
        o = sb("o", [128, GROUPS, PT])
        inv_sum = sb("inv_sum", [128, GROUPS, PT])
        h2 = sb("h2", [HALF, TILES, C])
        xn2 = sb("xn2", [HALF, TILES, C])
        x2t = sb("x2t", [128, 2, PT])
        sig = sb("sig", [HALF, 3, TILES, EXPERTS])
        picked = sb("picked", [HALF, TILES, EXPERTS])
        top = sb("top", [HALF, TILES, 8])
        top_at = sb("top_at", [HALF, TILES, 8], u32)
        top_no = sb("top_no", [HALF, TILES, 8])
        hot = sb("hot", [HALF, 2, TILES, EXPERTS])
        kept = sb("kept", [HALF, 2, TILES, EXPERTS])
        weight_sum = sb("weight_sum", [HALF, 3, TILES])
        comb = sb("comb", [HALF, TILES, EXPERTS])
        comb_t = sb("comb_t", [EXPERTS, PT])
        r = sb("r", [128, 2, PT])
        cr = sb("cr", [128, 2, PT])
        hid = sb("hid", [128, HT, PT])
        spacer = sb("spacer", [HALF, 1])
        y = sb("y", [HALF, TILES, C])

        bank = [ctx.enter_context(nc.psum_tensor(f"bank{i}", [128, 512], f32)) for i in range(8)]
        SCORE, PROBT, OUT, FC, GATE = (0, 1), (2, 3), (4, 5), 6, 7

        weights_in = sem("weights_in")
        x_in = sem("x_in")
        y_free = sem("y_free")
        rpe_ready, bias_w_ready, bias_w_in = sem("rpe_ready"), sem("bias_w_ready"), sem("bias_w_in")
        v_padded = sem("v_padded")
        tok_ready, h_ready, h_pb_ready = sem("tok_ready"), sem("h_ready"), sem("h_pb_ready")
        stats_ready, moments_ready, var_ready, rstd_ready, xn_ready = (
            sem("stats_ready"), sem("moments_ready"), sem("var_ready"), sem("rstd_ready"), sem("xn_ready"))
        xt_ready, xt_in = sem("xt_ready"), sem("xt_in")
        qk_ready, qk_in, v_ready, v_in = sem("qk_ready"), sem("qk_in"), sem("v_ready"), sem("v_in")
        scores_ready, biased, max_ready, probs_ready = (
            sem("scores_ready"), sem("biased"), sem("max_ready"), sem("probs_ready"))
        probst_ready, probst_in, pv_done, o_in = sem("probst_ready"), sem("probst_in"), sem("pv_done"), sem("o_in")
        sums_ready, inv_ready, o_normed = sem("sums_ready"), sem("inv_ready"), sem("o_normed")
        proj_ready, h2_ready = sem("proj_ready"), sem("h2_ready")
        x2t_ready, x2t_in, logits_ready, exp_ready = (
            sem("x2t_ready"), sem("x2t_in"), sem("logits_ready"), sem("exp_ready"))
        routing = sem("routing")
        comb_ready, combt_ready, combt_in = sem("comb_ready"), sem("combt_ready"), sem("combt_in")
        fc_ready, gate_ready, r_ready, cr_ready, hid_ready = (
            sem("fc_ready"), sem("gate_ready"), sem("r_ready"), sem("cr_ready"), sem("hid_ready"))
        y_ready, y_in = sem("y_ready"), sem("y_in")

        loads = [(w_tok, "w_tok"), (b_tok, "b_tok"), (w_qk, "w_qk"), (w_qo, "w_qo"), (rpe_m, "rpe_m"),
                 (rpe_f, "rpe_f"), (k_far, "k_far"), (w_proj, "w_proj"),
                 (b_proj, "b_proj"), (w_fc, "w_fc"), (w_out, "w_out"), (w_rt, "w_rt"), (b_rt, "b_rt"),
                 (masks, "masks"), (ident, "ident"), (rowsum_sel, "rowsum_sel"), (expert_sel, "expert_sel"),
                 (expert_no, "expert_no")]
        ALL_IN = 16 * (len(loads) + 1)
        STEPS = HT

        block = ctx.enter_context(nc.Block())

        def iterations(eng, step):
            step(0, True, False)
            with eng.Fori(1, PAIRS) as p:
                step(p, True, True)
            step(PAIRS, False, True)

        @block.sync
        def _(sp):
            sp.dma_start(x[:], a["x"][0]).then_inc(x_in, 16)
            for tile, name in loads:
                sp.dma_start(tile[:], a[name]).then_inc(weights_in, 16)
            sp.dma_start(w_vd[:, :, 0:C], a["w_v"]).then_inc(weights_in, 16)

            def load(p):
                sp.wait_ge(tok_ready, 2 * p)
                sp.dma_start(x[:], a["x"][bass.ds(p, 1)].rearrange("o q k t -> q (o k) t")).then_inc(x_in, 16)

            def store(f):
                sp.wait_ge(y_in, 2 * f + 2)
                sp.dma_start(out[bass.ds(f, 1)].rearrange("o i q c -> q (o i) c"), y[:]).then_inc(y_free, 16)

            load(1)
            with sp.Fori(1, PAIRS - 1) as p:
                load(p + 1)
                store(p - 1)
            store(PAIRS - 2)
            store(PAIRS - 1)
            sp.wait_ge(y_free, 16 * PAIRS + 16)

        @block.gpsimd
        def _(pool):
            pool.memset(minus_half[:], -0.5).then_inc(v_padded, 1)
            pool.memset(v[:], 0.0).then_inc(v_padded, 1)
            pool.wait_ge(v_padded, 2)
            pool.memset(v[:, :, :, HD:HD + 1], 1.0).then_inc(v_padded, 1)
            pool.wait_ge(weights_in, ALL_IN)

            def inverse_std(n):
                pool.wait_ge(var_ready, n + 1)
                pool.tensor_tensor(rstd[:], var_eps[:], minus_half[:], ALU.pow).then_inc(rstd_ready, 1)

            def step(p, attention, experts):
                f = p - 1
                if attention:
                    inverse_std(2 * p)
                    pool.wait_ge(h_ready, 2 * p + 2)
                    pool.wait_ge(h2_ready, 2 * p) if experts else None
                    pool.tensor_tensor(h_pb[:], h[:], b_proj[:], ALU.add).then_inc(h_pb_ready, 1)
                if experts:
                    for j in range(HT):
                        rows = 128 if j < HT - 1 else HID - 128 * (HT - 1)
                        pool.wait_ge(r_ready, HT * f + j + 1)
                        if j < RT:
                            pool.wait_ge(cr_ready, RT * f + j + 1)
                        left = cr if j < RT else r
                        pool.tensor_tensor(hid[0:rows, j, :], left[0:rows, j % 2, :], r[0:rows, j % 2, :],
                                           ALU.mult).then_inc(hid_ready, 1)
                if attention:
                    inverse_std(2 * p + 1)

            iterations(pool, step)

        @block.scalar
        def _(act):
            act.wait_ge(weights_in, ALL_IN)

            def step(p, attention, experts):
                f = p - 1
                if experts:
                    for c, n in ((0, CLO), (1, CHI)):
                        act.wait_ge(x2t_ready, 2 * f + c + 1)
                        nc.scalar.copy(x2t[0:n, c, :], bank[FC + c][0:n, 0:PT]).then_inc(x2t_in, 1)
                if attention:
                    for c, n in ((0, CLO), (1, CHI)):
                        act.wait_ge(xt_ready, 2 * p + c + 1)
                        nc.scalar.copy(xt[0:n, c, :], bank[PROBT[c]][0:n, 0:PT]).then_inc(xt_in, 1)
                if experts:
                    act.wait_ge(logits_ready, f + 1)
                    nc.scalar.activation(sig[:, 0].rearrange("q t e -> q (t e)"), bank[FC][0:HALF, 0:TILES * EXPERTS], ACT.Exp,
                                         scale=-1.0).then_inc(exp_ready, 1)
                if attention:
                    for g in range(2 * GROUPS):
                        act.wait_ge(qk_ready, 2 * GROUPS * p + g + 1)
                        if g < GROUPS:
                            nc.scalar.copy(qk[:, g, :], bank[SCORE[g % 2]][:, 0:PT]).then_inc(qk_in, 1)
                        else:
                            nc.scalar.activation(qk[:, g, :], bank[SCORE[g % 2]][:, 0:PT], ACT.Identity,
                                                 bias=k_far[:, 0:1]).then_inc(qk_in, 1)
                for u in range(STEPS):
                    if experts:
                        rows = 128 if u < HT - 1 else HID - 128 * (HT - 1)
                        act.wait_ge(fc_ready, HT * f + u + 1)
                        if u >= 2 or attention:
                            act.wait_ge(hid_ready, HT * f + u - 1) if not (u < 2) else None
                        nc.scalar.activation(r[0:rows, u % 2, :], bank[FC][0:rows, 0:PT],
                                             ACT.Relu).then_inc(r_ready, 1)
                    if attention and 1 <= u <= UNITS:
                        w = u - 1
                        for half in range(2):
                            act.wait_ge(probst_ready, 2 * UNITS * p + 2 * w + half + 1)
                            if experts or w >= 2:
                                act.wait_ge(pv_done, UNITS * p + w - 1)
                            nc.scalar.copy(probs_t[:, w % 2, half].rearrange("q e t -> q (e t)"),
                                           bank[PROBT[half]][0:HALF, 0:PT]).then_inc(probst_in, 1)
                    if attention and u < UNITS:
                        for e in range(2):
                            act.wait_ge(max_ready, 2 * UNITS * p + 2 * u + e + 1)
                            if experts or u >= 2:
                                act.wait_ge(probst_ready, 2 * UNITS * p + 2 * (u - 1))
                            for half in range(2):
                                last = nc.scalar.activation(
                                    probs[:, u % 2, e, half, :],
                                    bank[SCORE[e]][0:HALF, half * TOKENS:(half + 1) * TOKENS],
                                    ACT.Exp, bias=neg_max[:, u % 2, e, half:half + 1])
                            last.then_inc(probs_ready, 1)

            iterations(act, step)

        @block.vector
        def _(dve):
            nc.vector.memset(spacer[:], 0.0).then_inc(y_free, 16)
            dve.wait_ge(weights_in, ALL_IN)
            nc.vector.tensor_tensor(rpe_d[:], rpe_m[:], rpe_f[:], ALU.subtract).then_inc(rpe_ready, 1)
            dve.wait_ge(rpe_ready, 1)
            nc.vector.tensor_scalar(rpe_d[:], rpe_d[:], HD ** -0.5, None, ALU.mult).then_inc(rpe_ready, 1)
            nc.vector.tensor_scalar(w_qk[:, :, 0:GROUPS, :], w_qk[:, :, 0:GROUPS, :], HD ** -0.5, None,
                                    ALU.mult).then_inc(rpe_ready, 1)
            for c, n in ((0, CLO), (1, CHI)):
                dve.wait_ge(bias_w_ready, c + 1)
                nc.vector.tensor_copy(w_vd[0:n, c, C:VD], bank[c][0:n, 0:HEADS * NEAR]).then_inc(bias_w_in, 1)
            dve.wait_ge(v_padded, 3)

            def normalise(n, src, dst):
                for t in range(TILES):
                    last = nc.vector.bn_stats(stats[:, t, :], src[:, t, :])
                last.then_inc(stats_ready, 1)
                dve.wait_ge(weights_in, ALL_IN)
                dve.wait_ge(stats_ready, n + 1)
                for t in range(TILES):
                    last = nc.vector.bn_aggr(moments[:, t, :], stats[:, t, :])
                last.then_inc(moments_ready, 1)
                dve.wait_ge(moments_ready, n + 1)
                nc.vector.tensor_scalar(var_eps[:], moments[:, :, 1], EPS, None, ALU.add).then_inc(var_ready, 1)
                dve.wait_ge(rstd_ready, n + 1)
                for t in range(TILES):
                    last = nc.vector.tensor_scalar(dst[:, t, :], src[:, t, :], moments[:, t, 0:1], rstd[:, t:t + 1],
                                                   ALU.subtract, ALU.mult)
                last.then_inc(xn_ready, 1)

            def route(f):
                n = [11 * f]

                def then(ins, ahead_of_max=False):
                    n[0] = n[0] + 1
                    ins.then_inc(routing, 1)
                    dve.wait_ge(routing, n[0])
                    if ahead_of_max:
                        nc.vector.memset(spacer[:], 0.0)

                dve.wait_ge(exp_ready, f + 1)
                then(nc.vector.tensor_scalar(sig[:, 1], sig[:, 0], 1.0, None, ALU.add))
                then(nc.vector.reciprocal(sig[:, 2], sig[:, 1]))
                then(nc.vector.tensor_tensor(picked[:], sig[:, 2], b_rt[:], ALU.add), ahead_of_max=True)
                for t in range(TILES):
                    last = nc.vector.max(top[:, t, :], picked[:, t, :])
                then(last, ahead_of_max=True)
                for t in range(TILES):
                    last = nc.vector.max_index(top_at[:, t, :], top[:, t, :], picked[:, t, :])
                then(last)
                then(nc.vector.tensor_copy(top_no[:], top_at[:]))
                for k in range(2):
                    last = nc.vector.tensor_tensor(hot[:, k], expert_no[:], top_no[:, :, k:k + 1].to_broadcast([HALF, TILES, EXPERTS]),
                                                   ALU.is_equal)
                then(last)
                then(nc.vector.tensor_tensor(kept[:, 0], hot[:, 0], hot[:, 1], ALU.add))
                then(nc.vector.tensor_tensor(kept[:, 1], kept[:, 0], sig[:, 2], ALU.mult))
                then(nc.vector.tensor_reduce(weight_sum[:, 0], kept[:, 1], AX.X, ALU.add))
                nc.vector.tensor_scalar(weight_sum[:, 1], weight_sum[:, 0], 1e-20, None, ALU.add).then_inc(routing, 1)
                return 11 * f + 11

            def route_end(f):
                nc.vector.reciprocal(weight_sum[:, 2], weight_sum[:, 1]).then_inc(comb_ready, 1)
                dve.wait_ge(comb_ready, 2 * f + 1)
                nc.vector.tensor_tensor(comb[:], kept[:, 1], weight_sum[:, 2].unsqueeze(2).to_broadcast([HALF, TILES, EXPERTS]),
                                        ALU.mult).then_inc(comb_ready, 1)

            def step(p, attention, experts):
                f = p - 1
                if attention:
                    for b in range(2):
                        dve.wait_ge(tok_ready, 2 * p + b + 1)
                        if experts:
                            dve.wait_ge(h_pb_ready, p)
                        nc.vector.tensor_tensor(
                            h[:, 2 * b:2 * b + 2, :], bank[SCORE[b]][0:HALF, 0:2 * C].rearrange("q (t c) -> q t c", t=2),
                            b_tok[:], ALU.add).then_inc(h_ready, 1)
                    dve.wait_ge(h_ready, 2 * p + 2)
                    normalise(2 * p, h, xn)
                if experts:
                    dve.wait_ge(routing, route(f))
                    route_end(f)
                if attention:
                    for b in range(2):
                        dve.wait_ge(v_ready, 2 * p + b + 1)
                        rows = bank[PROBT[b]][0:HALF, 0:2 * VD].rearrange("q (t c) -> q t c", t=2)
                        for t in range(2):
                            nc.vector.tensor_copy(v[:, 2 * b + t, :, 0:HD],
                                                  rows[:, t, 0:C].rearrange("q (e d) -> q e d", d=HD))
                        nc.vector.tensor_copy(diff[:, 2 * b:2 * b + 2, :], rows[:, :, C:VD]).then_inc(v_in, 1)
                    dve.wait_ge(v_in, 2 * p + 2)
                if experts:
                    dve.wait_ge(combt_ready, f + 1)
                    nc.vector.tensor_copy(comb_t[:], bank[GATE][0:EXPERTS, 0:PT]).then_inc(combt_in, 1)
                for u in range(STEPS):
                    if attention and u < UNITS:
                        img, hp = divmod(u, HEADS // 2)
                        for e in range(2):
                            s = bank[SCORE[e]][0:HALF, 0:PT].rearrange("q (i t) -> q i t", i=2)
                            done = 2 * UNITS * p + 2 * u + e
                            dve.wait_ge(scores_ready, done + 1)
                            for i, m in enumerate((2, 1, 0)):
                                for half in range(2):
                                    lo, hi = window(half, m)
                                    if i:
                                        dve.wait_ge(biased, 6 * done + 2 * i + half - 1)
                                    nc.vector.scalar_tensor_tensor(
                                        out=s[:, half, lo:hi], in0=masks[:, half, m, lo:hi],
                                        scalar=diff[:, 2 * img + half, (2 * hp + e) * NEAR + m:(2 * hp + e) * NEAR + m + 1],
                                        in1=s[:, half, lo:hi], op0=ALU.mult, op1=ALU.add).then_inc(biased, 1)
                            dve.wait_ge(biased, 6 * done + 6)
                            nc.vector.tensor_reduce(neg_max[:, u % 2, e, :], s, AX.X, ALU.max,
                                                    negate=True).then_inc(max_ready, 1)
                    if experts and u < RT:
                        dve.wait_ge(gate_ready, RT * f + u + 1)
                        dve.wait_ge(r_ready, HT * f + u + 1)
                        if u >= 2:
                            dve.wait_ge(hid_ready, HT * f + u - 1)
                        nc.vector.tensor_tensor(cr[:, u % 2, :], bank[GATE][:, 0:PT], r[:, u % 2, :],
                                                ALU.mult).then_inc(cr_ready, 1)
                    if attention and u >= 3 and u % 2 == 1:
                        n = (u - 3) // 2
                        img, g = divmod(n, GROUPS)
                        dve.wait_ge(pv_done, UNITS * p + 2 * n + 2)
                        nc.vector.tensor_copy(o[:, g, img * TOKENS:(img + 1) * TOKENS],
                                              bank[OUT[n % 2]][:, 0:TOKENS]).then_inc(o_in, 1)
                if experts:
                    for b in range(2):
                        dve.wait_ge(y_ready, 2 * f + b + 1)
                        dve.wait_ge(y_free, 16 * f + 16)
                        nc.vector.tensor_tensor(y[:, 2 * b:2 * b + 2, :],
                                                bank[FC + b][0:HALF, 0:2 * C].rearrange("q (t c) -> q t c", t=2),
                                                h2[:, 2 * b:2 * b + 2, :], ALU.add).then_inc(y_in, 1)
                if attention:
                    for g in range(GROUPS):
                        dve.wait_ge(sums_ready, GROUPS * p + g + 1)
                        nc.vector.reciprocal(inv_sum[:, g, :], bank[SCORE[g % 2]][:, 0:PT]).then_inc(inv_ready, 1)
                    for g in range(GROUPS):
                        dve.wait_ge(inv_ready, GROUPS * p + g + 1)
                        nc.vector.tensor_tensor(o[:, g, :], o[:, g, :], inv_sum[:, g, :], ALU.mult).then_inc(o_normed, 1)
                    for b in range(2):
                        dve.wait_ge(proj_ready, 2 * p + b + 1)
                        dve.wait_ge(h_pb_ready, p + 1)
                        nc.vector.tensor_tensor(h2[:, 2 * b:2 * b + 2, :],
                                                bank[PROBT[b]][0:HALF, 0:2 * C].rearrange("q (t c) -> q t c", t=2),
                                                h_pb[:, 2 * b:2 * b + 2, :], ALU.add).then_inc(h2_ready, 1)
                    dve.wait_ge(h2_ready, 2 * p + 2)
                    normalise(2 * p + 1, h2, xn2)

            iterations(dve, step)

        @block.tensor
        def _(pe):
            pe.wait_ge(weights_in, ALL_IN)
            pe.wait_ge(rpe_ready, 3)
            for c, n in ((0, CLO), (1, CHI)):
                for k, kn in ((0, CLO), (1, CHI)):
                    last = nc.tensor.matmul(bank[c][0:n, 0:HEADS * NEAR], w_qo[0:kn, k, c * CLO:c * CLO + n],
                                            rpe_d[0:kn, k, :], start=k == 0, stop=k == 1)
                last.then_inc(bias_w_ready, 1)
            pe.wait_ge(bias_w_in, 2)
            pe.wait_ge(v_padded, 3)

            def transposes(src, banks, ready):
                for c, n in ((0, CLO), (1, CHI)):
                    for t in range(TILES):
                        last = nc.tensor.transpose(bank[banks[c]][0:n, t * HALF:(t + 1) * HALF],
                                                   src[:, t, c * CLO:c * CLO + n], ident[0:HALF, 0:HALF])
                    last.then_inc(ready, 1)

            def step(p, attention, experts):
                f = p - 1
                if attention:
                    pe.wait_ge(x_in, 16 * p + 16)
                    for b in range(2):
                        if experts:
                            pe.wait_ge(inv_ready, GROUPS * p)
                        for t in (2 * b, 2 * b + 1):
                            for k in range(KX):
                                last = nc.tensor.matmul(bank[SCORE[b]][0:HALF, (t % 2) * C:(t % 2 + 1) * C],
                                                        x[:, k, t * HALF:(t + 1) * HALF], w_tok[:, k, :],
                                                        start=k == 0, stop=k == KX - 1)
                        last.then_inc(tok_ready, 1)
                if experts:
                    pe.wait_ge(xn_ready, 2 * f + 2)
                    transposes(xn2, (FC, GATE), x2t_ready)
                if attention:
                    pe.wait_ge(xn_ready, 2 * p + 1)
                    if experts:
                        pe.wait_ge(h2_ready, 2 * p)
                    transposes(xn, PROBT, xt_ready)
                if experts:
                    pe.wait_ge(x2t_in, 2 * f + 2)
                    for t in range(TILES):
                        for c, n in ((0, CLO), (1, CHI)):
                            last = nc.tensor.matmul(bank[FC][0:HALF, t * EXPERTS:(t + 1) * EXPERTS],
                                                    x2t[0:n, c, t * HALF:(t + 1) * HALF], w_rt[0:n, c, :],
                                                    start=c == 0, stop=c == 1)
                    last.then_inc(logits_ready, 1)
                if attention:
                    pe.wait_ge(xt_in, 2 * p + 2)
                    for g in range(2 * GROUPS):
                        if g < 2:
                            pe.wait_ge(h_ready, 2 * p + g + 1)
                        else:
                            pe.wait_ge(qk_in, 2 * GROUPS * p + g - 1)
                        for c, n in ((0, CLO), (1, CHI)):
                            last = nc.tensor.matmul(bank[SCORE[g % 2]][:, 0:PT], w_qk[0:n, c, g, :], xt[0:n, c, :],
                                                    start=c == 0, stop=c == 1)
                        last.then_inc(qk_ready, 1)
                    for b in range(2):
                        for t in (2 * b, 2 * b + 1):
                            for c, n in ((0, CLO), (1, CHI)):
                                last = nc.tensor.matmul(bank[PROBT[b]][0:HALF, (t % 2) * VD:(t % 2 + 1) * VD],
                                                        xt[0:n, c, t * HALF:(t + 1) * HALF], w_vd[0:n, c, :],
                                                        start=c == 0, stop=c == 1)
                        last.then_inc(v_ready, 1)
                if experts:
                    pe.wait_ge(comb_ready, 2 * f + 2)
                    for t in range(TILES):
                        last = nc.tensor.transpose(bank[GATE][0:EXPERTS, t * HALF:(t + 1) * HALF], comb[:, t, :],
                                                   ident[0:HALF, 0:HALF])
                    last.then_inc(combt_ready, 1)
                if attention:
                    pe.wait_ge(qk_in, 2 * GROUPS * (p + 1))

                def scores(u, e):
                    img, hp = divmod(u, HEADS // 2)
                    if u:
                        pe.wait_ge(probs_ready, 2 * UNITS * p + 2 * u + e - 1)
                    g, q = divmod(2 * hp + e, 4)
                    at = slice(q * SLOT, q * SLOT + HD)
                    for half in range(2):
                        first = img * TOKENS + half * HALF
                        last = nc.tensor.matmul(bank[SCORE[e]][0:HALF, half * TOKENS:(half + 1) * TOKENS],
                                                qk[at, g, first:first + HALF],
                                                qk[at, GROUPS + g, img * TOKENS:(img + 1) * TOKENS],
                                                start=True, stop=True)
                    last.then_inc(scores_ready, 1)

                def hidden(u):
                    rows = 128 if u < HT - 1 else HID - 128 * (HT - 1)
                    if u:
                        pe.wait_ge(r_ready, HT * f + u)
                    for c, n in ((0, CLO), (1, CHI)):
                        last = nc.tensor.matmul(bank[FC][0:rows, 0:PT], w_fc[0:n, c, u * 128:u * 128 + rows],
                                                x2t[0:n, c, :], start=c == 0, stop=c == 1)
                    last.then_inc(fc_ready, 1)

                def gates(u):
                    pe.wait_ge(combt_in, f + 1)
                    if u:
                        pe.wait_ge(cr_ready, RT * f + u)
                    nc.tensor.matmul(bank[GATE][:, 0:PT], expert_sel[:, u, :], comb_t[:], start=True,
                                     stop=True).then_inc(gate_ready, 1)

                def probs_transposed(u):
                    pe.wait_ge(probs_ready, 2 * UNITS * p + 2 * u + 2)
                    for jt in range(2):
                        if u:
                            pe.wait_ge(probst_in, 2 * UNITS * p + 2 * u + jt - 1)
                        else:
                            pe.wait_ge(v_in, 2 * p + 2)
                        for e in range(2):
                            for half in range(2):
                                first = e * TOKENS + half * HALF
                                last = nc.tensor.transpose(bank[PROBT[jt]][0:HALF, first:first + HALF],
                                                           probs[:, u % 2, e, half, jt * HALF:(jt + 1) * HALF],
                                                           ident[0:HALF, 0:HALF])
                        last.then_inc(probst_ready, 1)

                def values(u):
                    img, hp = divmod(u, HEADS // 2)
                    n = img * GROUPS + hp // 2
                    pe.wait_ge(probst_in, 2 * UNITS * p + 2 * u + 2)
                    if hp % 2 == 0 and (experts or n >= 2):
                        pe.wait_ge(o_in, OGROUPS * p + n - 1)
                    for e in range(2):
                        head = 2 * hp + e
                        q = head % 4
                        for jt in range(2):
                            last = nc.tensor.matmul(bank[OUT[n % 2]][q * SLOT:(q + 1) * SLOT, 0:TOKENS],
                                                    v[:, 2 * img + jt, head, :], probs_t[:, u % 2, jt, e, :],
                                                    start=jt == 0, stop=jt == 1)
                    last.then_inc(pv_done, 1)

                for u in range(STEPS):
                    if attention and u < UNITS:
                        scores(u, 0)
                    if experts:
                        hidden(u)
                        if u < RT:
                            gates(u)
                    if attention:
                        if u < UNITS:
                            scores(u, 1)
                        if 1 <= u <= UNITS:
                            probs_transposed(u - 1)
                        if u >= 2:
                            values(u - 2)
                if experts:
                    pe.wait_ge(hid_ready, HT * (f + 1))
                    for b in range(2):
                        for t in (2 * b, 2 * b + 1):
                            for j in range(HT):
                                rows = 128 if j < HT - 1 else HID - 128 * (HT - 1)
                                last = nc.tensor.matmul(bank[FC + b][0:HALF, (t % 2) * C:(t % 2 + 1) * C],
                                                        hid[0:rows, j, t * HALF:(t + 1) * HALF], w_out[0:rows, j, :],
                                                        start=j == 0, stop=j == HT - 1)
                        last.then_inc(y_ready, 1)
                if attention:
                    pe.wait_ge(probs_ready, 2 * UNITS * (p + 1))
                    for g in range(GROUPS):
                        pe.wait_ge(o_in, OGROUPS * p + GROUPS + g + 1)
                        if g == 2:
                            pe.wait_ge(inv_ready, GROUPS * p + 1)
                        nc.tensor.matmul(bank[SCORE[g % 2]][:, 0:PT], rowsum_sel[:], o[:, g, :], start=True,
                                         stop=True).then_inc(sums_ready, 1)
                    pe.wait_ge(o_normed, GROUPS * (p + 1))
                    for b in range(2):
                        for t in (2 * b, 2 * b + 1):
                            for g in range(GROUPS):
                                last = nc.tensor.matmul(bank[PROBT[b]][0:HALF, (t % 2) * C:(t % 2 + 1) * C],
                                                        o[:, g, t * HALF:(t + 1) * HALF], w_proj[:, g, :],
                                                        start=g == 0, stop=g == GROUPS - 1)
                        last.then_inc(proj_ready, 1)

            iterations(pe, step)


def lay_out(i):
    f = np.float32

    def two(w):
        r = np.zeros((128, 2) + w.shape[1:], f)
        r[:, 0] = w[:CLO]
        r[:CHI, 1] = w[CLO:]
        return r

    r = {}
    x = i["x"].reshape(PAIRS, 2, CHANNELS, GRID, PATCH, GRID, PATCH).transpose(0, 2, 4, 6, 1, 3, 5)
    r["x"] = np.ascontiguousarray(x.reshape(PAIRS, KX, 128, PT).transpose(0, 2, 1, 3))
    r["w_tok"] = np.ascontiguousarray(i["L0_tok_W"].T.reshape(KX, 128, C).transpose(1, 0, 2))
    r["b_tok"] = np.ascontiguousarray(np.broadcast_to(i["L0_tok_b"], (HALF, 2, C)))
    w = i["L0_attn_qkv_w"]
    qk = np.zeros((C, 2 * GROUPS, 4, SLOT), f)
    qk[..., :HD] = w[:2 * C].T.reshape(C, 2 * GROUPS, 4, HD)
    r["w_qk"] = two(qk.reshape(C, 2 * GROUPS, 128))
    r["w_qo"] = two(w[:C])
    r["w_v"] = two(np.ascontiguousarray(w[2 * C:].T))
    rpe = i["L0_attn_rpe_w"]
    near, far = np.zeros((HEADS, HD, HEADS, NEAR), f), np.zeros((HEADS, HD, HEADS, NEAR), f)
    k_far = np.zeros((4, SLOT), f)
    k_far[:, :HD] = rpe[:, NEAR]
    for n in range(HEADS):
        near[n, :, n, :] = rpe[:, :NEAR]
        far[n, :, n, :] = rpe[:, NEAR:NEAR + 1]
    r["rpe_m"], r["rpe_f"] = two(near.reshape(C, -1)), two(far.reshape(C, -1))
    r["k_far"] = k_far.reshape(128, 1)
    proj = np.zeros((GROUPS, 4, SLOT, C), f)
    proj[:, :, :HD] = i["L0_attn_proj_w"].T.reshape(GROUPS, 4, HD, C)
    r["w_proj"] = np.ascontiguousarray(proj.reshape(GROUPS, 128, C).transpose(1, 0, 2))
    r["b_proj"] = np.ascontiguousarray(np.broadcast_to(i["L0_attn_proj_b"], (HALF, TILES, C)))
    fc = np.zeros((C, HT * 128), f)
    fc[:, :EXPERTS * C] = i["L0_ffn_w1"].transpose(1, 0, 2).reshape(C, EXPERTS * C)
    fc[:, EXPERTS * C:HID] = i["L0_ffn_w_fc_sh"]
    r["w_fc"] = two(fc)
    wo = np.zeros((HT * 128, C), f)
    wo[:EXPERTS * C] = i["L0_ffn_w2"].reshape(EXPERTS * C, C)
    wo[EXPERTS * C:HID] = i["L0_ffn_w_proj_sh"]
    r["w_out"] = np.ascontiguousarray(wo.reshape(HT, 128, C).transpose(1, 0, 2))
    r["w_rt"] = two(np.ascontiguousarray(i["L0_ffn_router_w"].T))
    r["b_rt"] = np.ascontiguousarray(np.broadcast_to(i["L0_ffn_balance_bias"], (HALF, TILES, EXPERTS)))
    b = buckets().reshape(2, HALF, TOKENS)
    r["masks"] = np.ascontiguousarray(np.stack([b == m for m in range(NEAR)], 2).transpose(1, 0, 2, 3).astype(f))
    r["ident"] = np.eye(128, dtype=f)
    sel = np.zeros((128, 128), f)
    for m in range(128):
        sel[m // SLOT * SLOT + HD, m] = 1
    r["rowsum_sel"] = sel
    e = np.arange(RT * 128) // C
    r["expert_sel"] = (np.arange(EXPERTS)[:, None] == e[None]).astype(f).reshape(EXPERTS, RT, 128)
    r["expert_no"] = np.ascontiguousarray(np.broadcast_to(np.arange(EXPERTS, dtype=f), (HALF, TILES, EXPERTS)))
    return r


def kernel(**inputs):
    import concourse.bacc as bacc
    from concourse.bass_utils import run_bass_kernel_spmd

    arrays = lay_out({k: np.asarray(v) for k, v in inputs.items()})
    nc = bacc.Bacc("TRN2", target_bir_lowering=False, num_devices=1)
    args = {k: nc.dram_tensor(f"in_{k}", v.shape, mybir.dt.from_np(v.dtype), kind="ExternalInput").ap()
            for k, v in arrays.items()}
    out = nc.dram_tensor("out", (PAIRS, TILES, HALF, C), mybir.dt.float32, kind="ExternalOutput").ap()
    vit_kernel(nc, args, out)
    got = run_bass_kernel_spmd(nc, [{f"in_{k}": v for k, v in arrays.items()}], core_ids=[0])
    return got.results[0]["out"].reshape(IMAGES, TOKENS, C)
```

```python
import numpy as np
import concourse.bass as bass
from concourse import mybir
from concourse.alu_op_type import AluOpType as ALU
from contextlib import ExitStack

IMAGES, CHANNELS, SIDE = 64, 3, 224
GRID = 14
PATCH = SIDE // GRID
TOKENS = GRID * GRID
C = 192
HEADS = 12
HD = C // HEADS
EXPERTS = 8
EPS = 1e-5

PAIRS = IMAGES // 2
HALF = TOKENS // 2
TILES = 4
PT = 2 * TOKENS
KX = CHANNELS * PATCH * PATCH // 128
CLO = 128
CHI = C - CLO
SLOT = 32
GROUPS = HEADS // 4
NEAR = 3
VD = C + HEADS * NEAR
HID = (EXPERTS + 1) * C
HT = (HID + 127) // 128
CD = C + CHI
RT = EXPERTS * C // 128
UNITS = 2 * HEADS // 2
OGROUPS = 2 * GROUPS
SHARED_AT = RT
HIDDEN_ORDER = [*range(SHARED_AT, HT), *range(RT)]
EARLY = HT - RT
PROBT_LAG, VALUE_LAG = 2, 4
HID_BUFS = 10
HID_REUSED = HT - HID_BUFS
SLOTS = UNITS + VALUE_LAG
LOW_CHI, LOW_HD, LOW_EXPERT, LOW_HEAD = range(4)


def buckets():
    alpha, beta, gamma = 1.9, 3.8, 15.2
    at = np.stack(np.meshgrid(np.arange(GRID), np.arange(GRID), indexing="ij"), -1).reshape(-1, 2).astype(np.float64)
    far = np.round(np.sqrt(((at[:, None] - at[None]) ** 2).sum(-1)))
    log = np.minimum(np.round(alpha + np.log(np.maximum(far, 1e-09) / alpha) / np.log(gamma / alpha) * (beta - alpha)), beta)
    b = np.where(far <= alpha, np.round(far).astype(np.int64), log.astype(np.int64))
    return b - b.min()


def window(half, bucket):
    b = buckets()[half * HALF:(half + 1) * HALF]
    cols = np.nonzero((b == bucket).any(0))[0]
    return int(cols.min()), int(cols.max()) + 1


def vit_kernel(nc, a, out):
    f32 = mybir.dt.float32
    f32r = mybir.dt.float32r
    u32 = mybir.dt.uint32
    ACT = mybir.ActivationFunctionType
    AX = mybir.AxisListType
    ctx = ExitStack()
    with ctx:
        def sb(name, shape, dt=f32):
            return ctx.enter_context(nc.sbuf_tensor(name, shape, dt))

        def sem(name):
            return ctx.enter_context(nc.semaphore(name))

        w_tok = sb("w_tok", [128, KX, C])
        b_tok = sb("b_tok", [HALF, 1, C])
        w_qk = sb("w_qk", [128, 2, 2, 2 * GROUPS * 128], f32r)
        k_far = sb("k_far", [128, 1])
        w_vd = sb("w_vd", [128, 2, 2, VD], f32r)
        w_proj = sb("w_proj", [128, GROUPS, C])
        b_proj = sb("b_proj", [HALF, 1, C])
        w_fc = sb("w_fc", [128, 2, 2, HT * 128], f32r)
        w_out = sb("w_out", [128, HT, C])
        w_rt_in = sb("w_rt_in", [128, 2, EXPERTS])
        w_rt = sb("w_rt", [128, 2, 2, EXPERTS], f32r)
        b_rt = sb("b_rt", [HALF, TILES, EXPERTS])
        masks = sb("masks", [HALF, 2, NEAR, TOKENS], mybir.dt.uint8)
        ident = sb("ident", [128, 128])
        selectors = sb("selectors", [SLOT + 2 * HEADS, RT * 128], f32r)
        low_rows = sb("low_rows", [128, 4])
        expert_no = sb("expert_no", [HALF, TILES, EXPERTS])
        minus_half = sb("minus_half", [HALF, TILES])
        x = sb("x", [128, KX, PT])
        h = sb("h", [HALF, TILES, C])
        h_pb = sb("h_pb", [HALF, TILES, C])
        stats = sb("stats", [HALF, TILES, 6])
        moments = sb("moments", [HALF, TILES, 2])
        var_eps = sb("var_eps", [HALF, TILES])
        rstd = sb("rstd", [HALF, TILES])
        xn = sb("xn", [HALF, TILES, CD])
        xt = sb("xt", [128, 3, PT], f32r)
        q = sb("q", [128, GROUPS, PT], f32r)
        k = sb("k", [128, 2, GROUPS, PT], f32r)
        v = sb("v", [HALF, TILES, HEADS, 4 * SLOT], f32r)
        diff = sb("diff", [HALF, TILES, HEADS * NEAR])
        probs = sb("probs", [HALF, 3, 2, 2, TOKENS])
        neg_max = sb("neg_max", [HALF, 2, 2, 2])
        prob_sum = sb("prob_sum", [HALF, TILES, HEADS])
        inv_sum = sb("inv_sum", [HALF, TILES, 2, HEADS])
        probs_t = sb("probs_t", [HALF, 2, 2 * TOKENS])
        probs_th = sb("probs_th", [HALF, 2, 2, 2 * TOKENS], f32r)
        probs_tl = sb("probs_tl", [HALF, 2, 2, 2 * TOKENS], f32r)
        o = sb("o", [128, GROUPS, PT])
        h2 = sb("h2", [HALF, TILES, C])
        xn2 = sb("xn2", [HALF, TILES, CD])
        x2t = sb("x2t", [128, 3, PT], f32r)
        high = sb("high", [128, PT], f32r)
        sig = sb("sig", [HALF, 3, TILES, EXPERTS])
        picked = sb("picked", [HALF, TILES, EXPERTS])
        top = sb("top", [HALF, TILES, 8])
        top_at = sb("top_at", [HALF, TILES, 8], u32)
        top_no = sb("top_no", [HALF, TILES, 8])
        hot = sb("hot", [HALF, 2, TILES, EXPERTS])
        kept = sb("kept", [HALF, 2, TILES, EXPERTS])
        weight_sum = sb("weight_sum", [HALF, 3, TILES])
        comb = sb("comb", [HALF, TILES, 2, EXPERTS])
        gates_t = sb("gates_t", [SLOT + 2 * HEADS, PT], f32r)
        r = sb("r", [128, 2, PT])
        gate = sb("gate", [128, PT])
        cr = sb("cr", [128, PT])
        hid = sb("hid", [128, HID_BUFS, PT])
        y = sb("y", [HALF, TILES, C])
        spacer = sb("spacer", [HALF, 1])

        comb_t, inv_t = gates_t[0:2 * EXPERTS, :], gates_t[SLOT:SLOT + 2 * HEADS, :]
        expert_sel = selectors[0:2 * EXPERTS, :].rearrange("q (j n) -> q j n", j=RT)
        head_sel = selectors[SLOT:SLOT + 2 * HEADS, 0:GROUPS * 128].rearrange("q (g n) -> q g n", g=GROUPS)
        nothing = selectors[0:1, C:3 * C]
        xt_high = k[:, 1, GROUPS - 1, :]
        q_high = k[:, 1]

        bank = [ctx.enter_context(nc.psum_tensor(f"bank{i}", [128, 512], f32)) for i in range(8)]
        SCORE, PROBT, OUT, FC, GATE, Y = (0, 1), 2, 3, 4, 5, (6, 7)
        TOK, QK, SPREAD = (FC, GATE), (PROBT, OUT, FC, GATE), (SCORE[1], SCORE[0], PROBT)

        weights_in = sem("weights_in")
        x_in = sem("x_in")
        y_free = sem("y_free")
        weights_split, bias_w_ready, bias_w_in = sem("weights_split"), sem("bias_w_ready"), sem("bias_w_in")
        v_padded = sem("v_padded")
        tok_ready, h_ready, h_pb_ready = sem("tok_ready"), sem("h_ready"), sem("h_pb_ready")
        stats_ready, moments_ready, var_ready, rstd_ready, xn_written, xn_ready = (
            [sem(name + which) for which in ("_1", "_2")]
            for name in ("stats_ready", "moments_ready", "var_ready", "rstd_ready", "xn_written", "xn_ready"))
        xt_ready, xt_high_in, xt_in = sem("xt_ready"), sem("xt_high_in"), sem("xt_in")
        qk_ready, qk_high_in, qk_in = sem("qk_ready"), sem("qk_high_in"), sem("qk_in")
        v_ready, v_high_in, v_in = sem("v_ready"), sem("v_high_in"), sem("v_in")
        scores_ready, scores_in, biased, max_ready, probs_ready = (
            sem("scores_ready"), sem("scores_in"), sem("biased"), sem("max_ready"), sem("probs_ready"))
        probst_ready, probst_in, probs_low_ready = sem("probst_ready"), sem("probst_in"), sem("probs_low_ready")
        pv_done, o_in = sem("pv_done"), sem("o_in")
        inv_half, inv_ready, invt_ready, inv_high_in, inv_in = (
            sem("inv_half"), sem("inv_ready"), sem("invt_ready"), sem("inv_high_in"), sem("inv_in"))
        inv_spread, o_normed = sem("inv_spread"), sem("o_normed")
        proj_ready, h2_ready = sem("proj_ready"), sem("h2_ready")
        x2t_ready, x2t_high_in, x2t_in, logits_ready, exp_ready = (
            sem("x2t_ready"), sem("x2t_high_in"), sem("x2t_in"), sem("logits_ready"), sem("exp_ready"))
        routing = sem("routing")
        comb_ready, combt_ready, comb_high_in, combt_in = (
            sem("comb_ready"), sem("combt_ready"), sem("comb_high_in"), sem("combt_in"))
        fc_ready, gate_ready, gate_in, r_ready, cr_ready, hid_ready, hid_used = (
            sem("fc_ready"), sem("gate_ready"), sem("gate_in"), sem("r_ready"), sem("cr_ready"), sem("hid_ready"),
            sem("hid_used"))
        y_ready, y_in = sem("y_ready"), sem("y_in")

        fc_in = hid[:].rearrange("q j t -> q (j t)")[:, 0:2 * HT * 128]
        qk_in_raw = x[:].rearrange("q k t -> q (k t)")[:, 0:4 * GROUPS * 128]
        selectors_in = probs[:].rearrange("q a b c t -> q (a b c t)")[0:SLOT + 2 * HEADS, 0:RT * 128]
        masks_in = [t[:].rearrange("q t c -> q (t c)")[:, 0:NEAR * TOKENS] for t in (h_pb, h2)]
        w_qo = r[:].rearrange("q a t -> q (a t)")[:, 0:2 * CD].rearrange("q (c n) -> q c n", c=2)
        rpe = cr[:, 0:6 * HEADS * NEAR].rearrange("q (a c n) -> q a c n", a=3, c=2)
        rpe_m, rpe_f, rpe_d = rpe[:, 0], rpe[:, 1], rpe[:, 2]
        w_vd_in = o[:].rearrange("q g t -> q (g t)")[:, 0:2 * VD].rearrange("q (c n) -> q c n", c=2)

        loads = [(w_tok[:], "w_tok"), (b_tok[:], "b_tok"), (qk_in_raw, "w_qk"), (w_qo, "w_qo"),
                 (rpe_m, "rpe_m"), (rpe_f, "rpe_f"), (k_far[:], "k_far"), (w_vd_in[:, :, 0:C], "w_v"),
                 (fc_in, "w_fc"), (w_rt_in[:], "w_rt"), (low_rows[:], "low_rows"),
                 (ident[:], "ident"), (selectors_in, "selectors"),
                 (expert_no[:], "expert_no"), (w_proj[:], "w_proj"), (b_proj[:], "b_proj"), (b_rt[:], "b_rt"),
                 (w_out[:], "w_out")]
        ALL_IN = 16 * (len(loads) + 2)
        PARTS = ((0, 128), (1, 128))

        def plain(ap):
            return ap.bitcast(f32)

        def rows_of(j):
            return 128 if j < HT - 1 else HID - 128 * (HT - 1)

        block = ctx.enter_context(nc.Block())

        def iterations(eng, step):
            step(0, True, False, True)
            with eng.Fori(1, PAIRS - 1) as p:
                step(p, True, True, True)
            step(PAIRS - 1, True, True, False)
            step(PAIRS, False, True, False)

        @block.sync
        def _(sp):
            for tile, name in loads:
                sp.dma_start(tile, a[name]).then_inc(weights_in, 16)
            for half in range(2):
                sp.dma_start(masks_in[half], a["masks"][:, half]).then_inc(weights_in, 16)

            sp.wait_ge(weights_split, 9)
            sp.dma_start(x[:], a["x"][0]).then_inc(x_in, 16)

            def load(p):
                sp.wait_ge(tok_ready, 2 * p)
                sp.dma_start(x[:], a["x"][bass.ds(p, 1)].rearrange("o q k t -> q (o k) t")).then_inc(x_in, 16)

            def store(f):
                sp.wait_ge(y_in, 2 * f + 2)
                sp.dma_start(out[bass.ds(f, 1)].rearrange("o i q c -> q (o i) c"), y[:]).then_inc(y_free, 16)

            load(1)
            with sp.Fori(1, PAIRS - 1) as p:
                load(p + 1)
                store(p - 1)
            store(PAIRS - 2)
            store(PAIRS - 1)
            sp.wait_ge(y_free, 16 * PAIRS + 16)

        @block.gpsimd
        def _(pool):
            pool.memset(minus_half[:], -0.5).then_inc(v_padded, 1)
            pool.wait_ge(weights_in, ALL_IN)
            pool.wait_ge(bias_w_in, 3)
            pool.memset(v[:].bitcast(f32), 0.0).then_inc(v_padded, 1)
            pool.wait_ge(v_padded, 2)

            def inverse_std(which, n):
                pool.wait_ge(var_ready[which], n + 1)
                pool.tensor_tensor(rstd[:], var_eps[:], minus_half[:], ALU.pow).then_inc(rstd_ready[which], 1)

            def hidden(f, n):
                rows = rows_of(HIDDEN_ORDER[n])
                pool.wait_ge(r_ready, HT * f + n + 1)
                relu = r[0:rows, n % 2, :]
                if n >= EARLY:
                    pool.wait_ge(gate_in, RT * f + n - EARLY + 1)
                    pool.wait_ge(hid_ready, HT * f + n)
                    pool.tensor_tensor(cr[:], gate[:], relu, ALU.mult).then_inc(cr_ready, 1)
                    pool.wait_ge(cr_ready, RT * f + n - EARLY + 1)
                if n >= HID_BUFS:
                    pool.wait_ge(hid_used, HID_REUSED * f + n - HID_BUFS + 1)
                pool.tensor_tensor(hid[0:rows, n % HID_BUFS, :], cr[0:rows] if n >= EARLY else relu, relu,
                                   ALU.mult).then_inc(hid_ready, 1)

            def low_probs(p, u, started):
                for jt in range(2):
                    pool.wait_ge(probst_in, 2 * UNITS * p + 2 * u + jt + 1)
                    if jt == 0 and (started or u >= 2):
                        pool.wait_ge(pv_done, UNITS * p + u - 1)
                    pool.tensor_tensor(probs_tl[:, u % 2, jt, :], probs_t[:, jt, :],
                                       plain(probs_th[:, u % 2, jt, :]), ALU.subtract).then_inc(probs_low_ready, 1)

            def step(p, attention, experts, following):
                f = p - 1
                if experts:
                    inverse_std(1, f)
                if attention:
                    pool.wait_ge(h_ready, 2 * p + 2)
                    if experts:
                        pool.wait_ge(h2_ready, 2 * p)
                    pool.tensor_tensor(h_pb[:], h[:], b_proj[:].to_broadcast([HALF, TILES, C]), ALU.add).then_inc(h_pb_ready, 1)
                if experts:
                    for n in range(EARLY):
                        hidden(f, n)
                for s in range(SLOTS):
                    if attention and 0 <= s - PROBT_LAG < UNITS:
                        low_probs(p, s - PROBT_LAG, experts)
                    if experts and s < RT:
                        hidden(f, s + EARLY)
                if following:
                    inverse_std(0, p + 1)

            inverse_std(0, 0)
            iterations(pool, step)

        @block.scalar
        def _(act):
            act.wait_ge(weights_in, ALL_IN)

            def relu(f, n):
                rows = rows_of(HIDDEN_ORDER[n])
                act.wait_ge(fc_ready, HT * f + n + 1)
                if n >= 2:
                    act.wait_ge(hid_ready, HT * f + n - 1)
                nc.scalar.activation(r[0:rows, n % 2, :], bank[FC][0:rows, 0:PT], ACT.Relu).then_inc(r_ready, 1)

            def xt_out(q):
                for c in range(2):
                    act.wait_ge(xt_ready, 2 * q + c + 1)
                    nc.scalar.copy(xt[:, 0, :] if c == 0 else xt_high, bank[TOK[c]][:, 0:PT]).then_inc(xt_high_in, 1)

            def step(p, attention, experts, following):
                f = p - 1
                if attention:
                    for g in range(2 * GROUPS):
                        act.wait_ge(qk_ready, 2 * GROUPS * p + g + 1)
                        value = bank[QK[g % len(QK)]][:, 0:PT]
                        if g < GROUPS:
                            nc.scalar.copy(q_high[:, g, :], value).then_inc(qk_high_in, 1)
                        else:
                            nc.scalar.activation(k[:, 0, g - GROUPS, :], value, ACT.Identity,
                                                 bias=k_far[:, 0:1]).then_inc(qk_high_in, 1)
                if experts:
                    for c in range(2):
                        act.wait_ge(x2t_ready, 2 * f + c + 1)
                        nc.scalar.copy(x2t[:, 0, :] if c == 0 else high[:], bank[SCORE[c]][:, 0:PT]).then_inc(x2t_high_in, 1)
                if attention:
                    for b in range(2):
                        act.wait_ge(v_ready, 2 * p + b + 1)
                        rows = bank[Y[b]][0:HALF, 0:2 * VD].rearrange("q (t c) -> q t c", t=2)
                        for e in range(4):
                            last = nc.scalar.copy(v[:, 2 * b:2 * b + 2, e::4, e * SLOT:e * SLOT + HD],
                                                  rows[:, :, 0:C].rearrange("q t (g e d) -> q t g e d", e=4, d=HD)[:, :, :, e, :])
                        last.then_inc(v_high_in, 1)
                if experts:
                    act.wait_ge(logits_ready, f + 1)
                    nc.scalar.activation(sig[:, 0].rearrange("q t e -> q (t e)"), bank[SCORE[0]][0:HALF, 0:TILES * EXPERTS],
                                         ACT.Exp, scale=-1.0).then_inc(exp_ready, 1)
                    for n in range(EARLY):
                        relu(f, n)

                def scores_out(s):
                    for e in range(2):
                        act.wait_ge(scores_ready, 2 * UNITS * p + 2 * s + e + 1)
                        if e == 0 and (experts or s >= 3):
                            act.wait_ge(probst_ready, 2 * UNITS * p + 2 * (s - 2))
                        nc.scalar.copy(probs[:, s % 3, e].rearrange("q i t -> q (i t)"),
                                       bank[SCORE[e]][0:HALF, 0:PT]).then_inc(scores_in, 1)

                def o_out(n):
                    img, g = divmod(n, GROUPS)
                    act.wait_ge(pv_done, UNITS * p + 2 * n + 2)
                    nc.scalar.copy(o[:, g, img * TOKENS:(img + 1) * TOKENS], bank[OUT][:, 0:TOKENS]).then_inc(o_in, 1)

                def exponentials(u, e):
                    img, hp = divmod(u, HEADS // 2)
                    act.wait_ge(max_ready, 2 * UNITS * p + 2 * u + e + 1)
                    for half in range(2):
                        last = nc.scalar.activation(
                            probs[:, u % 3, e, half, :], probs[:, u % 3, e, half, :], ACT.Exp,
                            bias=neg_max[:, u % 2, e, half:half + 1],
                            accum_out=prob_sum[:, 2 * img + half, 2 * hp + e:2 * hp + e + 1])
                    last.then_inc(probs_ready, 1)

                def probst_out(u, jt):
                    act.wait_ge(probst_ready, 2 * UNITS * p + 2 * u + jt + 1)
                    if jt == 0 and (experts or u >= 2):
                        act.wait_ge(pv_done, UNITS * p + u - 1)
                    nc.scalar.copy(probs_th[:, u % 2, jt, :], bank[PROBT][0:HALF, 0:PT])
                    if experts or u >= 1:
                        act.wait_ge(probs_low_ready, 2 * UNITS * p + 2 * (u - 1) + jt + 1)
                    nc.scalar.copy(probs_t[:, jt, :], bank[PROBT][0:HALF, 0:PT]).then_inc(probst_in, 1)

                def gate_out(i):
                    act.wait_ge(gate_ready, RT * f + i + 1)
                    if i:
                        act.wait_ge(cr_ready, RT * f + i)
                    nc.scalar.copy(gate[:], bank[GATE][:, 0:PT]).then_inc(gate_in, 1)

                for s in range(SLOTS):
                    if attention and s < UNITS:
                        scores_out(s)
                    if attention and s > VALUE_LAG and s % 2 == 1:
                        o_out((s - VALUE_LAG - 1) // 2)
                    if experts and s < RT:
                        relu(f, s + EARLY)
                    if experts and s == 0:
                        act.wait_ge(combt_ready, f + 1)
                        nc.scalar.copy(high[0:2 * EXPERTS, :], bank[GATE][0:2 * EXPERTS, 0:PT]).then_inc(comb_high_in, 1)
                    for i in range(2):
                        if attention and 0 <= s - PROBT_LAG < UNITS:
                            probst_out(s - PROBT_LAG, i)
                        if attention and 1 <= s <= UNITS:
                            exponentials(s - 1, i)
                    if experts and s < RT:
                        gate_out(s)
                    if attention and s == UNITS + 2:
                        act.wait_ge(invt_ready, p + 1)
                        nc.scalar.copy(high[0:2 * HEADS, :], bank[SCORE[0]][0:2 * HEADS, 0:PT]).then_inc(inv_high_in, 1)
                if following:
                    xt_out(p + 1)

            xt_out(0)
            iterations(act, step)

        @block.vector
        def _(dve):
            nc.vector.memset(spacer[:], 0.0).then_inc(y_free, 16)
            dve.wait_ge(weights_in, ALL_IN)
            nc.vector.tensor_tensor(rpe_d, rpe_m, rpe_f, ALU.subtract).then_inc(weights_split, 1)
            qk_raw = qk_in_raw.rearrange("q (c n) -> q c n", c=2)
            nc.vector.tensor_scalar(qk_raw[:, :, 0:GROUPS * 128], qk_raw[:, :, 0:GROUPS * 128], HD ** -0.5, None,
                                    ALU.mult).then_inc(weights_split, 1)
            dve.wait_ge(weights_split, 2)
            nc.vector.tensor_scalar(rpe_d, rpe_d, HD ** -0.5, None, ALU.mult).then_inc(weights_split, 1)
            fc_raw = fc_in.rearrange("q (c n) -> q c n", c=2)
            pairs = ((w_qk, qk_raw), (w_fc, fc_raw), (w_rt, w_rt_in[:]))
            nc.vector.tensor_copy(selectors[:], selectors_in)
            for half in range(2):
                nc.vector.tensor_copy(masks[:, half].rearrange("q m t -> q (m t)"), masks_in[half])
            for w, raw in pairs:
                nc.vector.tensor_copy(w[:, 0], raw).then_inc(weights_split, 1)
            dve.wait_ge(weights_split, 6)
            for w, raw in pairs:
                nc.vector.tensor_tensor(w[:, 1], raw, plain(w[:, 0]), ALU.subtract).then_inc(weights_split, 1)
            for c in range(2):
                dve.wait_ge(bias_w_ready, c + 1)
                nc.vector.tensor_copy(w_vd_in[:, c, C:VD], bank[c][:, 0:HEADS * NEAR]).then_inc(bias_w_in, 1)
            dve.wait_ge(bias_w_in, 2)
            nc.vector.tensor_copy(w_vd[:, 0], w_vd_in).then_inc(weights_split, 1)
            dve.wait_ge(weights_split, 10)
            nc.vector.tensor_tensor(w_vd[:, 1], w_vd_in, plain(w_vd[:, 0]), ALU.subtract).then_inc(bias_w_in, 1)

            def normalise_begin(which, n, src):
                for t in range(TILES):
                    last = nc.vector.bn_stats(stats[:, t, :], src[:, t, :])
                last.then_inc(stats_ready[which], 1)
                dve.wait_ge(stats_ready[which], n + 1)
                nc.vector.memset(spacer[:], 0.0)
                for t in range(TILES):
                    last = nc.vector.bn_aggr(moments[:, t, :], stats[:, t, :])
                last.then_inc(moments_ready[which], 1)
                dve.wait_ge(moments_ready[which], n + 1)
                nc.vector.tensor_scalar(var_eps[:], moments[:, :, 1], EPS, None, ALU.add).then_inc(var_ready[which], 1)

            def normalise_end(which, n, src, dst):
                dve.wait_ge(rstd_ready[which], n + 1)
                for t in range(TILES):
                    last = nc.vector.tensor_scalar(dst[:, t, 0:C], src[:, t, :], moments[:, t, 0:1], rstd[:, t:t + 1],
                                                   ALU.subtract, ALU.mult)
                last.then_inc(xn_written[which], 1)
                dve.wait_ge(xn_written[which], n + 1)
                nc.vector.tensor_copy(dst[:, :, C:CD], dst[:, :, CLO:C]).then_inc(xn_ready[which], 1)

            def low_part(out_ap, value, high):
                return nc.vector.tensor_tensor(out_ap, value, plain(high), ALU.subtract)

            def stack(out_ap, high, value, which, rows=128):
                return nc.vector.scalar_tensor_tensor(out=out_ap, in0=plain(high), scalar=low_rows[0:rows, which:which + 1],
                                                      in1=value, op0=ALU.mult, op1=ALU.add)

            def route(f):
                n = [11 * f]

                def then(ins, ahead_of_max=False):
                    n[0] = n[0] + 1
                    ins.then_inc(routing, 1)
                    dve.wait_ge(routing, n[0])
                    if ahead_of_max:
                        nc.vector.memset(spacer[:], 0.0)

                dve.wait_ge(exp_ready, f + 1)
                then(nc.vector.tensor_scalar(sig[:, 1], sig[:, 0], 1.0, None, ALU.add))
                then(nc.vector.reciprocal(sig[:, 2], sig[:, 1]))
                then(nc.vector.tensor_tensor(picked[:], sig[:, 2], b_rt[:], ALU.add), ahead_of_max=True)
                for t in range(TILES):
                    last = nc.vector.max(top[:, t, :], picked[:, t, :])
                then(last, ahead_of_max=True)
                for t in range(TILES):
                    last = nc.vector.max_index(top_at[:, t, :], top[:, t, :], picked[:, t, :])
                then(last)
                then(nc.vector.tensor_copy(top_no[:], top_at[:]))
                for best in range(2):
                    last = nc.vector.tensor_tensor(hot[:, best], expert_no[:],
                                                   top_no[:, :, best:best + 1].to_broadcast([HALF, TILES, EXPERTS]),
                                                   ALU.is_equal)
                then(last)
                then(nc.vector.tensor_tensor(kept[:, 0], hot[:, 0], hot[:, 1], ALU.add))
                then(nc.vector.tensor_tensor(kept[:, 1], kept[:, 0], sig[:, 2], ALU.mult))
                then(nc.vector.tensor_reduce(weight_sum[:, 0], kept[:, 1], AX.X, ALU.add))
                then(nc.vector.tensor_scalar(weight_sum[:, 1], weight_sum[:, 0], 1e-20, None, ALU.add))
                nc.vector.reciprocal(weight_sum[:, 2], weight_sum[:, 1]).then_inc(comb_ready, 1)
                dve.wait_ge(comb_ready, 3 * f + 1)
                for copy in range(2):
                    nc.vector.tensor_tensor(comb[:, :, copy, :], kept[:, 1],
                                            weight_sum[:, 2].unsqueeze(2).to_broadcast([HALF, TILES, EXPERTS]),
                                            ALU.mult).then_inc(comb_ready, 1)

            def h_from(q, b):
                dve.wait_ge(tok_ready, 2 * q + b + 1)
                nc.vector.tensor_tensor(
                    h[:, 2 * b:2 * b + 2, :], bank[TOK[b]][0:HALF, 0:2 * C].rearrange("q (t c) -> q t c", t=2),
                    b_tok[:].to_broadcast([HALF, 2, C]), ALU.add).then_inc(h_ready, 1)

            def xt_stacks(q):
                dve.wait_ge(xt_high_in, 2 * q + 1)
                low_part(xt[:, 1, :], bank[TOK[0]][:, 0:PT], xt[:, 0, :]).then_inc(xt_in, 1)
                dve.wait_ge(xt_high_in, 2 * q + 2)
                stack(xt[:, 2, :], xt_high, bank[TOK[1]][:, 0:PT], LOW_CHI).then_inc(xt_in, 1)

            def step(p, attention, experts, following):
                f = p - 1

                def qk_low(g):
                    dve.wait_ge(qk_high_in, 2 * GROUPS * p + g + 1)
                    value = bank[QK[g % len(QK)]][:, 0:PT]
                    if g < GROUPS:
                        stack(q[:, g, :], q_high[:, g, :], value, LOW_HD).then_inc(qk_in, 1)
                    else:
                        dve.wait_ge(qk_in, 2 * GROUPS * p + g - GROUPS + 1)
                        nc.vector.scalar_tensor_tensor(out=k[:, 1, g - GROUPS, :], in0=value, scalar=k_far[:, 0:1],
                                                       in1=plain(k[:, 0, g - GROUPS, :]), op0=ALU.add,
                                                       op1=ALU.subtract).then_inc(qk_in, 1)

                if experts:
                    dve.wait_ge(h2_ready, 2 * p)
                    normalise_begin(1, f, h2)
                if attention:
                    qk_low(0)
                if experts:
                    normalise_end(1, f, h2, xn2)
                if attention:
                    for g in range(1, 2 * GROUPS):
                        qk_low(g)
                if experts:
                    dve.wait_ge(x2t_high_in, 2 * f + 1)
                    low_part(x2t[:, 1, :], bank[SCORE[0]][:, 0:PT], x2t[:, 0, :]).then_inc(x2t_in, 1)
                    dve.wait_ge(x2t_high_in, 2 * f + 2)
                    stack(x2t[:, 2, :], high[:], bank[SCORE[1]][:, 0:PT], LOW_CHI).then_inc(x2t_in, 1)
                if attention:
                    for b in range(2):
                        dve.wait_ge(v_high_in, 2 * p + b + 1)
                        rows = bank[Y[b]][0:HALF, 0:2 * VD].rearrange("q (t c) -> q t c", t=2)
                        for e in range(4):
                            at = v[:, 2 * b:2 * b + 2, e::4, :]
                            low_part(at[:, :, :, e * SLOT + HD:(e + 1) * SLOT],
                                     rows[:, :, 0:C].rearrange("q t (g e d) -> q t g e d", e=4, d=HD)[:, :, :, e, :],
                                     at[:, :, :, e * SLOT:e * SLOT + HD])
                        nc.vector.tensor_copy(diff[:, 2 * b:2 * b + 2, :], rows[:, :, C:VD]).then_inc(v_in, 1)
                if experts:
                    route(f)
                if attention:
                    dve.wait_ge(v_in, 2 * p + 2)

                def bias_and_max(u, e):
                    img, hp = divmod(u, HEADS // 2)
                    sc = probs[:, u % 3, e]
                    done = 2 * UNITS * p + 2 * u + e
                    dve.wait_ge(scores_in, done + 1)
                    for i, m in enumerate((2, 1, 0)):
                        for half in range(2):
                            lo, hi = window(half, m)
                            if i:
                                dve.wait_ge(biased, 6 * done + 2 * i + half - 1)
                            at = (2 * hp + e) * NEAR + m
                            nc.vector.scalar_tensor_tensor(
                                out=sc[:, half, lo:hi], in0=masks[:, half, m, lo:hi],
                                scalar=diff[:, 2 * img + half, at:at + 1], in1=sc[:, half, lo:hi],
                                op0=ALU.mult, op1=ALU.add).then_inc(biased, 1)
                    dve.wait_ge(biased, 6 * done + 6)
                    nc.vector.tensor_reduce(neg_max[:, u % 2, e, :], sc, AX.X, ALU.max, negate=True).then_inc(max_ready, 1)

                for s in range(SLOTS):
                    if attention and s < UNITS:
                        bias_and_max(s, 0)
                    if experts and s == 0:
                        dve.wait_ge(comb_high_in, f + 1)
                        stack(comb_t, high[0:2 * EXPERTS, :], bank[GATE][0:2 * EXPERTS, 0:PT], LOW_EXPERT,
                              2 * EXPERTS).then_inc(combt_in, 1)
                    if attention and s < UNITS:
                        bias_and_max(s, 1)
                    if attention and s == UNITS + 1:
                        dve.wait_ge(probs_ready, 2 * UNITS * (p + 1))
                        nc.vector.reciprocal(inv_sum[:, :, 0, :], prob_sum[:]).then_inc(inv_half, 1)
                        dve.wait_ge(inv_half, p + 1)
                        nc.vector.tensor_copy(inv_sum[:, :, 1, :], inv_sum[:, :, 0, :]).then_inc(inv_ready, 1)
                    if following and s == UNITS + 1:
                        dve.wait_ge(h_pb_ready, p + 1)
                        h_from(p + 1, 0)
                    if following and s == UNITS + 2:
                        h_from(p + 1, 1)
                        dve.wait_ge(h_ready, 2 * p + 4)
                        normalise_begin(0, p + 1, h)
                    if experts and s == UNITS + 2:
                        for b in range(2):
                            dve.wait_ge(y_ready, 2 * f + b + 1)
                            if b == 0:
                                dve.wait_ge(y_free, 16 * f + 16)
                            nc.vector.tensor_tensor(y[:, 2 * b:2 * b + 2, :],
                                                    bank[Y[b]][0:HALF, 0:2 * C].rearrange("q (t c) -> q t c", t=2),
                                                    h2[:, 2 * b:2 * b + 2, :], ALU.add).then_inc(y_in, 1)
                    if attention and s == UNITS + 3:
                        dve.wait_ge(inv_high_in, p + 1)
                        stack(inv_t, high[0:2 * HEADS, :], bank[SCORE[0]][0:2 * HEADS, 0:PT], LOW_HEAD,
                              2 * HEADS).then_inc(inv_in, 1)
                    if following and s == UNITS + 3:
                        normalise_end(0, p + 1, h, xn)
                if attention:
                    for g in range(GROUPS):
                        dve.wait_ge(inv_spread, GROUPS * p + g + 1)
                        dve.wait_ge(o_in, OGROUPS * p + GROUPS + g + 1)
                        nc.vector.tensor_tensor(o[:, g, :], bank[SPREAD[g]][:, 0:PT], o[:, g, :],
                                                ALU.mult).then_inc(o_normed, 1)
                if following:
                    xt_stacks(p + 1)
                if attention:
                    for b in range(2):
                        dve.wait_ge(proj_ready, 2 * p + b + 1)
                        if experts:
                            dve.wait_ge(y_in, 2 * f + b + 1)
                        dve.wait_ge(h_pb_ready, p + 1)
                        nc.vector.tensor_tensor(h2[:, 2 * b:2 * b + 2, :],
                                                bank[Y[b]][0:HALF, 0:2 * C].rearrange("q (t c) -> q t c", t=2),
                                                h_pb[:, 2 * b:2 * b + 2, :], ALU.add).then_inc(h2_ready, 1)

            h_from(0, 0)
            h_from(0, 1)
            dve.wait_ge(h_ready, 2)
            normalise_begin(0, 0, h)
            normalise_end(0, 0, h, xn)
            xt_stacks(0)
            iterations(dve, step)

        @block.tensor
        def _(pe):
            pe.wait_ge(weights_in, ALL_IN)
            pe.wait_ge(weights_split, 3)
            for c in range(2):
                for kt, kn in ((0, CLO), (1, CHI)):
                    last = nc.tensor.matmul(bank[c][:, 0:HEADS * NEAR], w_qo[0:kn, kt, c * 128:(c + 1) * 128],
                                            rpe_d[0:kn, kt, :], start=kt == 0, stop=kt == 1)
                last.then_inc(bias_w_ready, 1)
            pe.wait_ge(bias_w_in, 3)
            pe.wait_ge(v_padded, 2)

            def transposes(src, banks, ready):
                for c in range(2):
                    for t in range(TILES):
                        last = nc.tensor.transpose(bank[banks[c]][:, t * HALF:(t + 1) * HALF],
                                                   src[:, t, c * 128:(c + 1) * 128], ident[0:HALF, 0:HALF])
                    last.then_inc(ready, 1)

            def channels(out_ap, w, xs, stationary_x):
                terms = ((w(0, 0), xs(0), 128), (w(0, 0), xs(1), 128), (w(1, 0), xs(0), 128),
                         (w(0, 1), xs(2), 128), (w(1, 1), xs(2), CHI))
                for i, (wa, xa, rows) in enumerate(terms):
                    left, right = (xa, wa) if stationary_x else (wa, xa)
                    last = nc.tensor.matmul(out_ap, left[0:rows], right[0:rows], start=i == 0, stop=i == len(terms) - 1)
                return last

            def patch_products(q, b):
                pe.wait_ge(x_in, 16 * q + 16)
                for t in (2 * b, 2 * b + 1):
                    for kt in range(KX):
                        last = nc.tensor.matmul(bank[TOK[b]][0:HALF, (t % 2) * C:(t % 2 + 1) * C],
                                                x[:, kt, t * HALF:(t + 1) * HALF], w_tok[:, kt, :],
                                                start=kt == 0, stop=kt == KX - 1)
                last.then_inc(tok_ready, 1)

            def x_transposed(q):
                pe.wait_ge(xn_ready[0], q + 1)
                transposes(xn, TOK, xt_ready)

            def step(p, attention, experts, following):
                f = p - 1
                if attention:
                    pe.wait_ge(xt_in, 2 * p + 2)
                    for g in range(2 * GROUPS):
                        if g >= len(QK):
                            pe.wait_ge(qk_in, 2 * GROUPS * p + g - len(QK) + 1)
                        channels(bank[QK[g % len(QK)]][:, 0:PT], lambda part, c: w_qk[:, part, c, g * 128:(g + 1) * 128],
                                 lambda i: xt[:, i, :], False).then_inc(qk_ready, 1)
                if experts:
                    pe.wait_ge(xn_ready[1], f + 1)
                    transposes(xn2, SCORE, x2t_ready)
                if attention:
                    if experts:
                        pe.wait_ge(h2_ready, 2 * p)
                    for b in range(2):
                        for t in (2 * b, 2 * b + 1):
                            last = channels(bank[Y[b]][0:HALF, (t % 2) * VD:(t % 2 + 1) * VD],
                                            lambda part, c: w_vd[:, part, c], lambda i: xt[:, i, t * HALF:(t + 1) * HALF],
                                            True)
                        last.then_inc(v_ready, 1)
                if experts:
                    pe.wait_ge(x2t_in, 2 * f + 2)
                    for t in range(TILES):
                        last = channels(bank[SCORE[0]][0:HALF, t * EXPERTS:(t + 1) * EXPERTS], lambda part, c: w_rt[:, part, c],
                                        lambda i: x2t[:, i, t * HALF:(t + 1) * HALF], True)
                    last.then_inc(logits_ready, 1)

                def hidden(n):
                    j, rows = HIDDEN_ORDER[n], rows_of(HIDDEN_ORDER[n])
                    if n or not attention:
                        pe.wait_ge(r_ready, HT * f + n)
                    else:
                        pe.wait_ge(qk_in, 2 * GROUPS * (p + 1))
                    channels(bank[FC][0:rows, 0:PT], lambda part, c: w_fc[:, part, c, j * 128:j * 128 + rows],
                             lambda i: x2t[:, i, :], False).then_inc(fc_ready, 1)

                if experts:
                    for n in range(EARLY):
                        hidden(n)
                if attention:
                    pe.wait_ge(qk_in, 2 * GROUPS * (p + 1))

                def scores(u, e):
                    img, hp = divmod(u, HEADS // 2)
                    if u:
                        pe.wait_ge(scores_in, 2 * UNITS * p + 2 * u + e - 1)
                    elif experts:
                        pe.wait_ge(exp_ready, f + 1)
                    g, slot = divmod(2 * hp + e, 4)
                    high = slice(slot * SLOT, slot * SLOT + HD)
                    both = slice(slot * SLOT, (slot + 1) * SLOT)
                    keys = slice(img * TOKENS, (img + 1) * TOKENS)
                    for half in range(2):
                        at = bank[SCORE[e]][0:HALF, half * TOKENS:(half + 1) * TOKENS]
                        queries = slice(img * TOKENS + half * HALF, img * TOKENS + (half + 1) * HALF)
                        nc.tensor.matmul(at, q[both, g, queries], k[both, 0, g, keys], start=True, stop=False)
                        last = nc.tensor.matmul(at, q[high, g, queries], k[high, 1, g, keys], start=False, stop=True)
                    last.then_inc(scores_ready, 1)

                def gates(i):
                    pe.wait_ge(combt_in, f + 1)
                    if i:
                        pe.wait_ge(gate_in, RT * f + i)
                    nc.tensor.matmul(bank[GATE][:, 0:PT], expert_sel[:, i, :], comb_t, start=True,
                                     stop=True).then_inc(gate_ready, 1)

                def probs_transposed(u, jt):
                    if jt == 0:
                        pe.wait_ge(probs_ready, 2 * UNITS * p + 2 * u + 2)
                    if u or jt:
                        pe.wait_ge(probst_in, 2 * UNITS * p + 2 * u + jt)
                    for e in range(2):
                        for half in range(2):
                            first = e * TOKENS + half * HALF
                            last = nc.tensor.transpose(bank[PROBT][0:HALF, first:first + HALF],
                                                       probs[:, u % 3, e, half, jt * HALF:(jt + 1) * HALF],
                                                       ident[0:HALF, 0:HALF])
                    last.then_inc(probst_ready, 1)

                def values(u):
                    img, hp = divmod(u, HEADS // 2)
                    n = img * GROUPS + hp // 2
                    pe.wait_ge(probs_low_ready, 2 * UNITS * p + 2 * u + 2)
                    if u == 0:
                        pe.wait_ge(v_in, 2 * p + 2)
                    if hp % 2 == 0 and n:
                        pe.wait_ge(o_in, OGROUPS * p + n)
                    terms = [(e, jt, part) for e in range(2) for jt in range(2) for part in (probs_th, probs_tl)]
                    for i, (e, jt, part) in enumerate(terms):
                        last = nc.tensor.matmul(bank[OUT][:, 0:TOKENS], v[:, 2 * img + jt, 2 * hp + e, :],
                                                part[:, u % 2, jt, e * TOKENS:(e + 1) * TOKENS],
                                                start=hp % 2 == 0 and i == 0, stop=hp % 2 == 1 and i == len(terms) - 1)
                    last.then_inc(pv_done, 1)

                def second_product(n, b):
                    j, rows = HIDDEN_ORDER[n], rows_of(HIDDEN_ORDER[n])
                    if b == 0:
                        pe.wait_ge(hid_ready, HT * f + n + 1)
                        if attention and n == 0:
                            pe.wait_ge(v_in, 2 * p + 2)
                    if n == 0:
                        nc.tensor.matmul(bank[Y[b]][0:HALF, 0:2 * C], nothing[:, 0:HALF], nothing, start=True, stop=False)
                    for t in (2 * b, 2 * b + 1):
                        last = nc.tensor.matmul(bank[Y[b]][0:HALF, (t % 2) * C:(t % 2 + 1) * C],
                                                hid[0:rows, n % HID_BUFS, t * HALF:(t + 1) * HALF], w_out[0:rows, j, :],
                                                start=False, stop=n == HT - 1 and t % 2 == 1)
                    if n == HT - 1:
                        last.then_inc(y_ready, 1)
                    elif b == 1 and n < HID_REUSED:
                        last.then_inc(hid_used, 1)

                for s in range(SLOTS):
                    if attention and s < UNITS:
                        scores(s, 0)
                        scores(s, 1)
                    if attention and s >= VALUE_LAG:
                        values(s - VALUE_LAG)
                    if experts and s < RT:
                        hidden(s + EARLY)
                    if attention and 0 <= s - PROBT_LAG < UNITS:
                        probs_transposed(s - PROBT_LAG, 0)
                    if experts and s == 0:
                        pe.wait_ge(comb_ready, 3 * f + 3)
                        if not attention:
                            pe.wait_ge(gate_in, RT * f)
                        for t in range(TILES):
                            last = nc.tensor.transpose(bank[GATE][0:2 * EXPERTS, t * HALF:(t + 1) * HALF],
                                                       comb[:, t].rearrange("q a e -> q (a e)"), ident[0:HALF, 0:HALF])
                        last.then_inc(combt_ready, 1)
                    if experts and s < HT:
                        second_product(s, 0)
                    if attention and 0 <= s - PROBT_LAG < UNITS:
                        probs_transposed(s - PROBT_LAG, 1)
                    if experts and s < RT:
                        gates(s)
                    if experts and s < HT:
                        second_product(s, 1)
                    if following and s in (UNITS, UNITS + 1):
                        if experts:
                            pe.wait_ge(r_ready, HT * (f + 1))
                            pe.wait_ge(gate_in, RT * (f + 1))
                        patch_products(p + 1, s - UNITS)
                    if attention and s == UNITS + 2:
                        pe.wait_ge(inv_ready, p + 1)
                        pe.wait_ge(scores_in, 2 * UNITS * (p + 1))
                        for t in range(TILES):
                            last = nc.tensor.transpose(bank[SCORE[0]][0:2 * HEADS, t * HALF:(t + 1) * HALF],
                                                       inv_sum[:, t].rearrange("q a e -> q (a e)"), ident[0:HALF, 0:HALF])
                        last.then_inc(invt_ready, 1)
                if attention:
                    pe.wait_ge(inv_in, p + 1)
                    pe.wait_ge(probst_in, 2 * UNITS * (p + 1))
                    for g in range(GROUPS):
                        nc.tensor.matmul(bank[SPREAD[g]][:, 0:PT], head_sel[:, g, :], inv_t, start=True,
                                         stop=True).then_inc(inv_spread, 1)
                if following:
                    x_transposed(p + 1)
                if attention:
                    pe.wait_ge(o_normed, GROUPS * (p + 1))
                    if experts:
                        pe.wait_ge(y_in, 2 * f + 2)
                    for b in range(2):
                        for t in (2 * b, 2 * b + 1):
                            for g in range(GROUPS):
                                last = nc.tensor.matmul(bank[Y[b]][0:HALF, (t % 2) * C:(t % 2 + 1) * C],
                                                        o[:, g, t * HALF:(t + 1) * HALF], w_proj[:, g, :],
                                                        start=g == 0, stop=g == GROUPS - 1)
                        last.then_inc(proj_ready, 1)

            patch_products(0, 0)
            patch_products(0, 1)
            x_transposed(0)
            iterations(pe, step)


def lay_out(i):
    f = np.float32

    def two(w):
        return np.ascontiguousarray(np.stack([w[:CLO], np.concatenate([w[CLO:], w[CLO:]])], 1))

    r = {}
    x = i["x"].reshape(PAIRS, 2, CHANNELS, GRID, PATCH, GRID, PATCH).transpose(0, 2, 4, 6, 1, 3, 5)
    r["x"] = np.ascontiguousarray(x.reshape(PAIRS, KX, 128, PT).transpose(0, 2, 1, 3))
    r["w_tok"] = np.ascontiguousarray(i["L0_tok_W"].T.reshape(KX, 128, C).transpose(1, 0, 2))
    r["b_tok"] = np.ascontiguousarray(np.broadcast_to(i["L0_tok_b"], (HALF, 1, C)))
    w = i["L0_attn_qkv_w"]
    qk = w[:2 * C].T.reshape(C, 2 * GROUPS, 4, HD)
    r["w_qk"] = two(np.concatenate([qk, qk], -1).reshape(C, -1)).reshape(128, -1)
    r["w_qo"] = two(np.concatenate([w[:C], w[:C, CLO:]], 1))
    r["w_v"] = two(np.ascontiguousarray(w[2 * C:].T))
    rpe = i["L0_attn_rpe_w"]
    near, far = np.zeros((HEADS, HD, HEADS, NEAR), f), np.zeros((HEADS, HD, HEADS, NEAR), f)
    k_far = np.ascontiguousarray(np.broadcast_to(rpe[:, NEAR], (4, 2, HD)))
    for n in range(HEADS):
        near[n, :, n, :] = rpe[:, :NEAR]
        far[n, :, n, :] = rpe[:, NEAR:NEAR + 1]
    r["rpe_m"], r["rpe_f"] = two(near.reshape(C, -1)), two(far.reshape(C, -1))
    r["k_far"] = k_far.reshape(128, 1)
    proj = np.zeros((GROUPS, 4, SLOT, C), f)
    proj[:, :, :HD] = proj[:, :, HD:] = i["L0_attn_proj_w"].T.reshape(GROUPS, 4, HD, C)
    r["w_proj"] = np.ascontiguousarray(proj.reshape(GROUPS, 128, C).transpose(1, 0, 2))
    r["b_proj"] = np.ascontiguousarray(np.broadcast_to(i["L0_attn_proj_b"], (HALF, 1, C)))
    fc = np.zeros((C, HT * 128), f)
    fc[:, :EXPERTS * C] = i["L0_ffn_w1"].transpose(1, 0, 2).reshape(C, EXPERTS * C)
    fc[:, EXPERTS * C:HID] = i["L0_ffn_w_fc_sh"]
    r["w_fc"] = two(fc).reshape(128, -1)
    wo = np.zeros((HT * 128, C), f)
    wo[:EXPERTS * C] = i["L0_ffn_w2"].reshape(EXPERTS * C, C)
    wo[EXPERTS * C:HID] = i["L0_ffn_w_proj_sh"]
    r["w_out"] = np.ascontiguousarray(wo.reshape(HT, 128, C).transpose(1, 0, 2))
    r["w_rt"] = two(np.ascontiguousarray(i["L0_ffn_router_w"].T))
    r["b_rt"] = np.ascontiguousarray(np.broadcast_to(i["L0_ffn_balance_bias"], (HALF, TILES, EXPERTS)))
    b = buckets().reshape(2, HALF, TOKENS)
    r["masks"] = np.ascontiguousarray(np.stack([b == m for m in range(NEAR)], 2).transpose(1, 0, 2, 3).reshape(HALF, 2, -1).astype(f))
    r["ident"] = np.eye(128, dtype=f)
    twice = lambda n: np.tile(np.arange(n), 2)[:, None]
    r["selectors"] = np.zeros((SLOT + 2 * HEADS, RT * 128), f)
    r["selectors"][:2 * EXPERTS] = twice(EXPERTS) == np.arange(RT * 128) // C
    r["selectors"][SLOT:, :GROUPS * 128] = twice(HEADS) == np.arange(GROUPS * 128) // SLOT
    row = np.arange(128)
    low = [row >= CHI, row % SLOT >= HD, row >= EXPERTS, row >= HEADS]
    r["low_rows"] = np.where(np.stack(low, 1), -1.0, 0.0).astype(f)
    r["expert_no"] = np.ascontiguousarray(np.broadcast_to(np.arange(EXPERTS, dtype=f), (HALF, TILES, EXPERTS)))
    return r


def kernel(**inputs):
    import concourse.bacc as bacc
    from concourse.bass_utils import run_bass_kernel_spmd

    arrays = lay_out({k: np.asarray(v) for k, v in inputs.items()})
    nc = bacc.Bacc("TRN2", target_bir_lowering=False, num_devices=1)
    args = {k: nc.dram_tensor(f"in_{k}", v.shape, mybir.dt.from_np(v.dtype), kind="ExternalInput").ap()
            for k, v in arrays.items()}
    out = nc.dram_tensor("out", (PAIRS, TILES, HALF, C), mybir.dt.float32, kind="ExternalOutput").ap()
    vit_kernel(nc, args, out)
    got = run_bass_kernel_spmd(nc, [{f"in_{k}": v for k, v in arrays.items()}], core_ids=[0])
    return got.results[0]["out"].reshape(IMAGES, TOKENS, C)
```

```python
import numpy as np
import concourse.bass as bass
from concourse import mybir
from concourse.alu_op_type import AluOpType as ALU
from contextlib import ExitStack

IMAGES, CHANNELS, SIDE = 64, 3, 224
GRID = 14
PATCH = SIDE // GRID
TOKENS = GRID * GRID
C = 192
HEADS = 12
HD = C // HEADS
EXPERTS = 8
EPS = 1e-5

PAIRS = IMAGES // 2
HALF = TOKENS // 2
TILES = 4
PT = 2 * TOKENS
KX = CHANNELS * PATCH * PATCH // 128
CLO = 128
CHI = C - CLO
SLOT = 32
GROUPS = HEADS // 4
NEAR = 3
VD = C + HEADS * NEAR
HID = (EXPERTS + 1) * C
HT = (HID + 127) // 128
CD = C + CHI
RT = EXPERTS * C // 128
UNITS = 2 * HEADS // 2
OGROUPS = 2 * GROUPS
BY_VECTOR = 3
SHARED_AT = RT
HIDDEN_ORDER = [*reversed(range(SHARED_AT, HT)), *range(RT)]
LAST_ROWS = HID - 128 * (HT - 1)
EARLY = HT - RT
PROBT_LAG, VALUE_LAG = 2, 4
HID_BUFS = 10
HID_REUSED = HT - HID_BUFS
SLOTS = UNITS + VALUE_LAG
LOW_CHI, LOW_HD, LOW_EXPERT, LOW_HEAD = range(4)


def buckets():
    alpha, beta, gamma = 1.9, 3.8, 15.2
    at = np.stack(np.meshgrid(np.arange(GRID), np.arange(GRID), indexing="ij"), -1).reshape(-1, 2).astype(np.float64)
    far = np.round(np.sqrt(((at[:, None] - at[None]) ** 2).sum(-1)))
    log = np.minimum(np.round(alpha + np.log(np.maximum(far, 1e-09) / alpha) / np.log(gamma / alpha) * (beta - alpha)), beta)
    b = np.where(far <= alpha, np.round(far).astype(np.int64), log.astype(np.int64))
    return b - b.min()


def window(half, bucket):
    b = buckets()[half * HALF:(half + 1) * HALF]
    cols = np.nonzero((b == bucket).any(0))[0]
    return int(cols.min()), int(cols.max()) + 1


def vit_kernel(nc, a, out):
    f32 = mybir.dt.float32
    f32r = mybir.dt.float32r
    u32 = mybir.dt.uint32
    ACT = mybir.ActivationFunctionType
    AX = mybir.AxisListType
    ctx = ExitStack()
    with ctx:
        def sb(name, shape, dt=f32):
            return ctx.enter_context(nc.sbuf_tensor(name, shape, dt))

        def sem(name):
            return ctx.enter_context(nc.semaphore(name))

        w_tok = sb("w_tok", [128, KX, C])
        b_tok = sb("b_tok", [HALF, 1, C])
        w_qk = sb("w_qk", [128, 2, 2, 2 * GROUPS * 128], f32r)
        k_far = sb("k_far", [128, 1])
        w_vd = sb("w_vd", [128, 2, 2, VD], f32r)
        w_proj = sb("w_proj", [128, GROUPS, C])
        b_proj = sb("b_proj", [HALF, 1, C])
        w_fc = sb("w_fc", [128, 2, 2, HT * 128], f32r)
        w_out = sb("w_out", [128, HT, C])
        b_rt = sb("b_rt", [HALF, TILES, EXPERTS])
        masks = sb("masks", [HALF, 2, NEAR, TOKENS], mybir.dt.uint8)
        ident = sb("ident", [128, 128])
        selectors = sb("selectors", [SLOT + 2 * HEADS, RT * 128], f32r)
        low_rows = sb("low_rows", [128, 4])
        expert_no = sb("expert_no", [HALF, TILES, EXPERTS])
        minus_half = sb("minus_half", [HALF, TILES])
        x = sb("x", [128, KX, PT])
        h = sb("h", [HALF, TILES, C])
        h_pb = sb("h_pb", [HALF, TILES, C])
        stats = sb("stats", [HALF, TILES, 6])
        moments = sb("moments", [HALF, TILES, 2])
        var_eps = sb("var_eps", [HALF, TILES])
        rstd = sb("rstd", [HALF, TILES])
        xn = sb("xn", [HALF, TILES, CD])
        xt = sb("xt", [128, 3, PT], f32r)
        q = sb("q", [128, GROUPS, PT], f32r)
        k = sb("k", [128, 2, GROUPS, PT], f32r)
        v = sb("v", [HALF, TILES, HEADS, 4 * SLOT], f32r)
        probs = sb("probs", [HALF, 3, 2, 2, TOKENS])
        neg_max = sb("neg_max", [HALF, 2, 2, 2])
        prob_sum = sb("prob_sum", [HALF, TILES, HEADS])
        inv_sum = sb("inv_sum", [HALF, TILES, 2, HEADS])
        probs_t = sb("probs_t", [HALF, 2, 2 * TOKENS])
        probs_th = sb("probs_th", [HALF, 2, 2, 2 * TOKENS], f32r)
        probs_tl = sb("probs_tl", [HALF, 2, 2, 2 * TOKENS], f32r)
        o = sb("o", [128, GROUPS, PT])
        h2 = sb("h2", [HALF, TILES, C])
        xn2 = sb("xn2", [HALF, TILES, CD])
        x2t = sb("x2t", [128, 3, PT], f32r)
        high = sb("high", [128, PT], f32r)
        sig = sb("sig", [HALF, 3, TILES, EXPERTS])
        picked = sb("picked", [HALF, TILES, EXPERTS])
        top = sb("top", [HALF, TILES, 8])
        top_at = sb("top_at", [HALF, TILES, 8], u32)
        top_no = sb("top_no", [HALF, TILES, 8])
        hot = sb("hot", [HALF, 2, TILES, EXPERTS])
        kept = sb("kept", [HALF, 2, TILES, EXPERTS])
        weight_sum = sb("weight_sum", [HALF, 3, TILES])
        comb = sb("comb", [HALF, TILES, 2, EXPERTS])
        gates_t = sb("gates_t", [SLOT + 2 * HEADS, PT], f32r)
        r = sb("r", [128, 2, PT])
        gate = sb("gate", [128, PT])
        cr = sb("cr", [128, PT])
        hid = sb("hid", [128, HID_BUFS, PT])
        y = sb("y", [HALF, TILES, C])
        one = sb("one", [HALF, 1])
        spacer = sb("spacer", [HALF, 1])

        v_raw, diff = xn[:, :, 0:VD], xn[:, :, C:VD]
        logits_t = cr[LAST_ROWS:LAST_ROWS + EXPERTS, :]
        comb_t, inv_t = gates_t[0:2 * EXPERTS, :], gates_t[SLOT:SLOT + 2 * HEADS, :]
        expert_sel = selectors[0:2 * EXPERTS, :].rearrange("q (j n) -> q j n", j=RT)
        head_sel = selectors[SLOT:SLOT + 2 * HEADS, 0:GROUPS * 128].rearrange("q (g n) -> q g n", g=GROUPS)
        nothing = selectors[0:1, C:3 * C]
        xt_high = k[:, 1, GROUPS - 1, :]
        q_high = k[:, 1]

        bank = [ctx.enter_context(nc.psum_tensor(f"bank{i}", [128, 512], f32)) for i in range(8)]
        SCORE, PROBT, OUT, FC, GATE, Y = (0, 1), 2, 3, 4, 5, (6, 7)
        TOK, QK, X2T, V, SPREAD = (FC, GATE), (PROBT, OUT, FC, GATE, *SCORE), (PROBT, OUT), (Y[0], OUT), (SCORE[1], SCORE[0], PROBT)

        weights_in = sem("weights_in")
        x_in = sem("x_in")
        y_free = sem("y_free")
        weights_split, bias_w_ready, bias_w_in = sem("weights_split"), sem("bias_w_ready"), sem("bias_w_in")
        v_padded = sem("v_padded")
        tok_ready, h_ready, h_pb_ready = sem("tok_ready"), sem("h_ready"), sem("h_pb_ready")
        stats_ready, moments_ready, var_ready, rstd_ready, xn_written, xn_ready = (
            [sem(name + which) for which in ("_1", "_2")]
            for name in ("stats_ready", "moments_ready", "var_ready", "rstd_ready", "xn_written", "xn_ready"))
        xt_ready, xt_high_in, xt_in = sem("xt_ready"), sem("xt_high_in"), sem("xt_in")
        qk_ready, qk_high_in, qk_in = sem("qk_ready"), sem("qk_high_in"), sem("qk_in")
        v_ready, v_raw_in, v_high_in, v_in = sem("v_ready"), sem("v_raw_in"), sem("v_high_in"), sem("v_in")
        scores_ready, scores_in, biased, max_ready, probs_ready = (
            sem("scores_ready"), sem("scores_in"), sem("biased"), sem("max_ready"), sem("probs_ready"))
        probst_ready, probst_in, probs_high_ready, probs_low_ready = (
            sem("probst_ready"), sem("probst_in"), sem("probs_high_ready"), sem("probs_low_ready"))
        pv_done, o_in = sem("pv_done"), sem("o_in")
        inv_half, inv_ready, invt_ready, inv_high_in, inv_in = (
            sem("inv_half"), sem("inv_ready"), sem("invt_ready"), sem("inv_high_in"), sem("inv_in"))
        inv_spread, o_normed = sem("inv_spread"), sem("o_normed")
        proj_ready, h2_ready = sem("proj_ready"), sem("h2_ready")
        x2t_ready, x2t_high_in, x2t_in, logits_in, logits_ready, exp_ready = (
            sem("x2t_ready"), sem("x2t_high_in"), sem("x2t_in"), sem("logits_in"), sem("logits_ready"), sem("exp_ready"))
        routing = sem("routing")
        comb_ready, combt_ready, comb_high_in, combt_in = (
            sem("comb_ready"), sem("combt_ready"), sem("comb_high_in"), sem("combt_in"))
        gated_ready = sem("gated_ready")
        fc_ready, gate_ready, gate_in, r_ready, cr_ready, hid_ready, hid_used = (
            sem("fc_ready"), sem("gate_ready"), sem("gate_in"), sem("r_ready"), sem("cr_ready"), sem("hid_ready"),
            sem("hid_used"))
        y_ready, y_in = sem("y_ready"), sem("y_in")

        fc_in = hid[:].rearrange("q j t -> q (j t)")[:, 0:2 * HT * 128]
        qk_in_raw = x[:].rearrange("q k t -> q (k t)")[:, 0:4 * GROUPS * 128]
        selectors_in = probs[:].rearrange("q a b c t -> q (a b c t)")[0:SLOT + 2 * HEADS, 0:RT * 128]
        masks_in = [t[:].rearrange("q t c -> q (t c)")[:, 0:NEAR * TOKENS] for t in (h_pb, h2)]
        w_qo = r[:].rearrange("q a t -> q (a t)")[:, 0:2 * CD].rearrange("q (c n) -> q c n", c=2)
        rpe = cr[:, 0:6 * HEADS * NEAR].rearrange("q (a c n) -> q a c n", a=3, c=2)
        rpe_m, rpe_f, rpe_d = rpe[:, 0], rpe[:, 1], rpe[:, 2]
        w_vd_in = o[:].rearrange("q g t -> q (g t)")[:, 0:2 * VD].rearrange("q (c n) -> q c n", c=2)

        loads = [(w_tok[:], "w_tok"), (b_tok[:], "b_tok"), (qk_in_raw, "w_qk"), (w_qo, "w_qo"),
                 (rpe_m, "rpe_m"), (rpe_f, "rpe_f"), (k_far[:], "k_far"), (w_vd_in[:, :, 0:C], "w_v"),
                 (fc_in, "w_fc"), (low_rows[:], "low_rows"),
                 (ident[:], "ident"), (selectors_in, "selectors"),
                 (expert_no[:], "expert_no"), (w_proj[:], "w_proj"), (b_proj[:], "b_proj"), (b_rt[:], "b_rt"),
                 (w_out[:], "w_out")]
        ALL_IN = 16 * (len(loads) + 2)
        PARTS = ((0, 128), (1, 128))

        def plain(ap):
            return ap.bitcast(f32)

        def by_vector(n):
            return n > EARLY and (n - EARLY) % BY_VECTOR == 0

        def relus(n):
            return sum(not by_vector(i) for i in range(n))

        RELUS = relus(HT)

        def fc_bank(n):
            return bank[GATE if n == 1 else FC]

        def rows_of(j):
            return 128 if j < HT - 1 else LAST_ROWS

        block = ctx.enter_context(nc.Block())

        def iterations(eng, step):
            step(0, True, False, True)
            with eng.Fori(1, PAIRS - 1) as p:
                step(p, True, True, True)
            step(PAIRS - 1, True, True, False)
            step(PAIRS, False, True, False)

        @block.sync
        def _(sp):
            for tile, name in loads:
                sp.dma_start(tile, a[name]).then_inc(weights_in, 16)
            for half in range(2):
                sp.dma_start(masks_in[half], a["masks"][:, half]).then_inc(weights_in, 16)

            sp.wait_ge(weights_split, 7)
            sp.dma_start(x[:], a["x"][0]).then_inc(x_in, 16)

            def load(p):
                sp.wait_ge(tok_ready, 2 * p)
                sp.dma_start(x[:], a["x"][bass.ds(p, 1)].rearrange("o q k t -> q (o k) t")).then_inc(x_in, 16)

            def store(f):
                sp.wait_ge(y_in, 2 * f + 2)
                sp.dma_start(out[bass.ds(f, 1)].rearrange("o i q c -> q (o i) c"), y[:]).then_inc(y_free, 16)

            load(1)
            with sp.Fori(1, PAIRS - 1) as p:
                load(p + 1)
                store(p - 1)
            store(PAIRS - 2)
            store(PAIRS - 1)
            sp.wait_ge(y_free, 16 * PAIRS + 16)

        @block.gpsimd
        def _(pool):
            pool.memset(minus_half[:], -0.5).then_inc(v_padded, 1)
            pool.memset(one[:], 1.0).then_inc(v_padded, 1)
            pool.wait_ge(weights_in, ALL_IN)
            pool.wait_ge(bias_w_in, 3)
            pool.memset(v[:].bitcast(f32), 0.0).then_inc(v_padded, 1)
            pool.wait_ge(v_padded, 3)

            def inverse_std(which, n):
                pool.wait_ge(var_ready[which], n + 1)
                pool.tensor_tensor(rstd[:], var_eps[:], minus_half[:], ALU.pow).then_inc(rstd_ready[which], 1)

            def hidden(f, n):
                if by_vector(n):
                    return
                rows = rows_of(HIDDEN_ORDER[n])
                pool.wait_ge(r_ready, RELUS * f + relus(n + 1))
                relu = r[0:rows, n % 2, :]
                left = relu
                if n >= EARLY:
                    pool.wait_ge(gate_in, RT * f + n - EARLY + 1)
                    pool.wait_ge(hid_ready, HT * f + n)
                    pool.tensor_tensor(cr[:], gate[:], relu, ALU.mult).then_inc(cr_ready, 1)
                    pool.wait_ge(cr_ready, (RELUS - EARLY) * f + relus(n + 1) - EARLY)
                    left = cr[:]
                if n >= HID_BUFS:
                    pool.wait_ge(hid_used, HID_REUSED * f + n - HID_BUFS + 1)
                pool.tensor_tensor(hid[0:rows, n % HID_BUFS, :], left[0:rows], relu, ALU.mult).then_inc(hid_ready, 1)

            def low_probs(p, u, jt, started):
                pool.wait_ge(probst_in, 2 * UNITS * p + 2 * u + jt + 1)
                if jt == 0 and (started or u >= 2):
                    pool.wait_ge(pv_done, UNITS * p + u - 1)
                if jt == 1:
                    pool.tensor_tensor(probs_th[:, u % 2, jt, :], probs_t[:, jt, :],
                                       one[:].to_broadcast([HALF, PT]), ALU.mult).then_inc(probs_high_ready, 1)
                    pool.wait_ge(probs_high_ready, UNITS * p + u + 1)
                pool.tensor_tensor(probs_tl[:, u % 2, jt, :], probs_t[:, jt, :],
                                   plain(probs_th[:, u % 2, jt, :]), ALU.subtract).then_inc(probs_low_ready, 1)

            def step(p, attention, experts, following):
                f = p - 1
                if experts:
                    inverse_std(1, f)
                if attention:
                    pool.wait_ge(h_ready, 2 * p + 2)
                    if experts:
                        pool.wait_ge(h2_ready, 2 * p)
                    pool.tensor_tensor(h_pb[:], h[:], b_proj[:].to_broadcast([HALF, TILES, C]), ALU.add).then_inc(h_pb_ready, 1)
                def v_low(b):
                    pool.wait_ge(v_high_in, 2 * p + b + 1)
                    for e in range(4):
                        at = v[:, 2 * b:2 * b + 2, e::4, :]
                        last = pool.tensor_tensor(
                            at[:, :, :, e * SLOT + HD:(e + 1) * SLOT],
                            v_raw[:, 2 * b:2 * b + 2, 0:C].rearrange("q t (g e d) -> q t g e d", e=4, d=HD)[:, :, :, e, :],
                            plain(at[:, :, :, e * SLOT:e * SLOT + HD]), ALU.subtract)
                    last.then_inc(v_in, 1)

                if attention:
                    v_low(0)
                if experts:
                    for n in range(EARLY):
                        hidden(f, n)
                for s in range(SLOTS):
                    if attention and 0 <= s - PROBT_LAG < UNITS:
                        low_probs(p, s - PROBT_LAG, 0, experts)
                    if experts and s < RT:
                        hidden(f, s + EARLY)
                    if attention and s == 1:
                        v_low(1)
                    if attention and 0 <= s - PROBT_LAG < UNITS:
                        low_probs(p, s - PROBT_LAG, 1, experts)
                if following:
                    inverse_std(0, p + 1)

            inverse_std(0, 0)
            iterations(pool, step)

        @block.scalar
        def _(act):
            act.wait_ge(weights_in, ALL_IN)

            def relu(f, n):
                rows = rows_of(HIDDEN_ORDER[n])
                act.wait_ge(fc_ready, HT * f + n + 1)
                if n >= 2:
                    act.wait_ge(hid_ready, HT * f + n - 1)
                nc.scalar.activation(r[0:rows, n % 2, :], fc_bank(n)[0:rows, 0:PT], ACT.Relu).then_inc(r_ready, 1)

            def xt_out(q):
                for c in range(2):
                    act.wait_ge(xt_ready, 2 * q + c + 1)
                    nc.scalar.copy(xt[:, 0, :] if c == 0 else xt_high, bank[TOK[c]][:, 0:PT]).then_inc(xt_high_in, 1)

            def step(p, attention, experts, following):
                f = p - 1

                def v_out(b):
                    act.wait_ge(v_ready, 2 * p + b + 1)
                    rows = bank[V[b]][0:HALF, 0:2 * VD].rearrange("q (t c) -> q t c", t=2)
                    nc.scalar.copy(v_raw[:, 2 * b:2 * b + 2, :], rows).then_inc(v_raw_in, 1)
                    for e in range(4):
                        last = nc.scalar.copy(v[:, 2 * b:2 * b + 2, e::4, e * SLOT:e * SLOT + HD],
                                              rows[:, :, 0:C].rearrange("q t (g e d) -> q t g e d", e=4, d=HD)[:, :, :, e, :])
                    last.then_inc(v_high_in, 1)

                if attention:
                    for g in range(2 * GROUPS):
                        act.wait_ge(qk_ready, 2 * GROUPS * p + g + 1)
                        value = bank[QK[g % len(QK)]][:, 0:PT]
                        if g < GROUPS:
                            nc.scalar.copy(q_high[:, g, :], value).then_inc(qk_high_in, 1)
                        else:
                            nc.scalar.activation(k[:, 0, g - GROUPS, :], value, ACT.Identity,
                                                 bias=k_far[:, 0:1]).then_inc(qk_high_in, 1)
                if experts:
                    for c in range(2):
                        act.wait_ge(x2t_ready, 2 * f + c + 1)
                        nc.scalar.copy(x2t[:, 0, :] if c == 0 else high[:], bank[X2T[c]][:, 0:PT]).then_inc(x2t_high_in, 1)
                if attention:
                    v_out(0)
                if experts:
                    act.wait_ge(fc_ready, HT * f + 1)
                    nc.scalar.copy(logits_t, bank[FC][LAST_ROWS:LAST_ROWS + EXPERTS, 0:PT]).then_inc(logits_in, 1)
                    relu(f, 0)
                    act.wait_ge(logits_ready, f + 1)
                    nc.scalar.activation(sig[:, 0].rearrange("q t e -> q (t e)"), bank[X2T[0]][0:HALF, 0:TILES * EXPERTS],
                                         ACT.Exp, scale=-1.0).then_inc(exp_ready, 1)
                    for n in range(1, EARLY):
                        relu(f, n)

                def scores_out(s):
                    for e in range(2):
                        act.wait_ge(scores_ready, 2 * UNITS * p + 2 * s + e + 1)
                        if e == 0 and (experts or s >= 3):
                            act.wait_ge(probst_ready, 2 * UNITS * p + 2 * (s - 2))
                        nc.scalar.copy(probs[:, s % 3, e].rearrange("q i t -> q (i t)"),
                                       bank[SCORE[e]][0:HALF, 0:PT]).then_inc(scores_in, 1)

                def o_out(n):
                    img, g = divmod(n, GROUPS)
                    act.wait_ge(pv_done, UNITS * p + 2 * n + 2)
                    nc.scalar.copy(o[:, g, img * TOKENS:(img + 1) * TOKENS], bank[OUT][:, 0:TOKENS]).then_inc(o_in, 1)

                def exponentials(u, e):
                    img, hp = divmod(u, HEADS // 2)
                    act.wait_ge(max_ready, 2 * UNITS * p + 2 * u + e + 1)
                    for half in range(2):
                        last = nc.scalar.activation(
                            probs[:, u % 3, e, half, :], probs[:, u % 3, e, half, :], ACT.Exp,
                            bias=neg_max[:, u % 2, e, half:half + 1],
                            accum_out=prob_sum[:, 2 * img + half, 2 * hp + e:2 * hp + e + 1])
                    last.then_inc(probs_ready, 1)

                def probst_out(u, jt):
                    act.wait_ge(probst_ready, 2 * UNITS * p + 2 * u + jt + 1)
                    if jt == 0:
                        if experts or u >= 2:
                            act.wait_ge(pv_done, UNITS * p + u - 1)
                        nc.scalar.copy(probs_th[:, u % 2, jt, :], bank[PROBT][0:HALF, 0:PT])
                    if experts or u >= 1:
                        act.wait_ge(probs_low_ready, 2 * UNITS * p + 2 * (u - 1) + jt + 1)
                    nc.scalar.copy(probs_t[:, jt, :], bank[PROBT][0:HALF, 0:PT]).then_inc(probst_in, 1)

                def gate_out(i):
                    act.wait_ge(gate_ready, RT * f + i + 1)
                    if i:
                        act.wait_ge(hid_ready, HT * f + EARLY + i)
                    nc.scalar.copy(gate[:], bank[GATE][:, 0:PT]).then_inc(gate_in, 1)

                if attention:
                    scores_out(0)
                for s in range(SLOTS):
                    for i in range(2):
                        if attention and 1 <= s <= UNITS:
                            exponentials(s - 1, i)
                        if experts and 1 < s < RT and i == 0:
                            gate_out(s)
                        if experts and s == 1 and i == 1:
                            gate_out(s)
                        if attention and 0 <= s - PROBT_LAG < UNITS:
                            probst_out(s - PROBT_LAG, i)
                        if i == 0:
                            if attention and s > VALUE_LAG and s % 2 == 1:
                                o_out((s - VALUE_LAG - 1) // 2)
                            if experts and s < RT and not by_vector(s + EARLY):
                                relu(f, s + EARLY)
                            if experts and s == 0:
                                act.wait_ge(combt_ready, f + 1)
                                nc.scalar.copy(high[0:2 * EXPERTS, :],
                                               bank[GATE][0:2 * EXPERTS, 0:PT]).then_inc(comb_high_in, 1)
                    if attention and s == 1:
                        v_out(1)
                    if attention and s + 1 < UNITS:
                        scores_out(s + 1)
                    if experts and s == 0:
                        gate_out(s)
                    if attention and s == UNITS + 1:
                        act.wait_ge(invt_ready, p + 1)
                        nc.scalar.copy(high[0:2 * HEADS, :], bank[SCORE[0]][0:2 * HEADS, 0:PT]).then_inc(inv_high_in, 1)
                if following:
                    xt_out(p + 1)

            xt_out(0)
            iterations(act, step)

        @block.vector
        def _(dve):
            nc.vector.memset(spacer[:], 0.0).then_inc(y_free, 16)
            dve.wait_ge(weights_in, ALL_IN)
            nc.vector.tensor_tensor(rpe_d, rpe_m, rpe_f, ALU.subtract).then_inc(weights_split, 1)
            qk_raw = qk_in_raw.rearrange("q (c n) -> q c n", c=2)
            nc.vector.tensor_scalar(qk_raw[:, :, 0:GROUPS * 128], qk_raw[:, :, 0:GROUPS * 128], HD ** -0.5, None,
                                    ALU.mult).then_inc(weights_split, 1)
            dve.wait_ge(weights_split, 2)
            nc.vector.tensor_scalar(rpe_d, rpe_d, HD ** -0.5, None, ALU.mult).then_inc(weights_split, 1)
            fc_raw = fc_in.rearrange("q (c n) -> q c n", c=2)
            pairs = ((w_qk, qk_raw), (w_fc, fc_raw))
            nc.vector.tensor_copy(selectors[:], selectors_in)
            for half in range(2):
                nc.vector.tensor_copy(masks[:, half].rearrange("q m t -> q (m t)"), masks_in[half])
            for w, raw in pairs:
                nc.vector.tensor_copy(w[:, 0], raw).then_inc(weights_split, 1)
            dve.wait_ge(weights_split, 5)
            for w, raw in pairs:
                nc.vector.tensor_tensor(w[:, 1], raw, plain(w[:, 0]), ALU.subtract).then_inc(weights_split, 1)
            for c in range(2):
                dve.wait_ge(bias_w_ready, c + 1)
                nc.vector.tensor_copy(w_vd_in[:, c, C:VD], bank[c][:, 0:HEADS * NEAR]).then_inc(bias_w_in, 1)
            dve.wait_ge(bias_w_in, 2)
            nc.vector.tensor_copy(w_vd[:, 0], w_vd_in).then_inc(weights_split, 1)
            dve.wait_ge(weights_split, 8)
            nc.vector.tensor_tensor(w_vd[:, 1], w_vd_in, plain(w_vd[:, 0]), ALU.subtract).then_inc(bias_w_in, 1)

            def statistics(which, src, b):
                for t in (2 * b, 2 * b + 1):
                    last = nc.vector.bn_stats(stats[:, t, :], src[:, t, :])
                last.then_inc(stats_ready[which], 1)

            def normalise_begin(which, n):
                dve.wait_ge(stats_ready[which], 2 * n + 2)
                nc.vector.memset(spacer[:], 0.0)
                for t in range(TILES):
                    last = nc.vector.bn_aggr(moments[:, t, :], stats[:, t, :])
                last.then_inc(moments_ready[which], 1)
                dve.wait_ge(moments_ready[which], n + 1)
                nc.vector.tensor_scalar(var_eps[:], moments[:, :, 1], EPS, None, ALU.add).then_inc(var_ready[which], 1)

            def normalise_end(which, n, src, dst):
                dve.wait_ge(rstd_ready[which], n + 1)
                for t in range(TILES):
                    last = nc.vector.tensor_scalar(dst[:, t, 0:C], src[:, t, :], moments[:, t, 0:1], rstd[:, t:t + 1],
                                                   ALU.subtract, ALU.mult)
                last.then_inc(xn_written[which], 1)
                dve.wait_ge(xn_written[which], n + 1)
                nc.vector.tensor_copy(dst[:, :, C:CD], dst[:, :, CLO:C]).then_inc(xn_ready[which], 1)

            def low_part(out_ap, value, high):
                return nc.vector.tensor_tensor(out_ap, value, plain(high), ALU.subtract)

            def stack(out_ap, high, value, which, rows=128):
                return nc.vector.scalar_tensor_tensor(out=out_ap, in0=plain(high), scalar=low_rows[0:rows, which:which + 1],
                                                      in1=value, op0=ALU.mult, op1=ALU.add)

            def route(f):
                n = [11 * f]

                def then(ins, ahead_of_max=False):
                    n[0] = n[0] + 1
                    ins.then_inc(routing, 1)
                    dve.wait_ge(routing, n[0])
                    if ahead_of_max:
                        nc.vector.memset(spacer[:], 0.0)

                dve.wait_ge(exp_ready, f + 1)
                then(nc.vector.tensor_scalar(sig[:, 1], sig[:, 0], 1.0, None, ALU.add))
                then(nc.vector.reciprocal(sig[:, 2], sig[:, 1]))
                then(nc.vector.tensor_tensor(picked[:], sig[:, 2], b_rt[:], ALU.add), ahead_of_max=True)
                for t in range(TILES):
                    last = nc.vector.max(top[:, t, :], picked[:, t, :])
                then(last, ahead_of_max=True)
                for t in range(TILES):
                    last = nc.vector.max_index(top_at[:, t, :], top[:, t, :], picked[:, t, :])
                then(last)
                then(nc.vector.tensor_copy(top_no[:], top_at[:]))
                for best in range(2):
                    last = nc.vector.tensor_tensor(hot[:, best], expert_no[:],
                                                   top_no[:, :, best:best + 1].to_broadcast([HALF, TILES, EXPERTS]),
                                                   ALU.is_equal)
                then(last)
                then(nc.vector.tensor_tensor(kept[:, 0], hot[:, 0], hot[:, 1], ALU.add))
                then(nc.vector.tensor_tensor(kept[:, 1], kept[:, 0], sig[:, 2], ALU.mult))
                then(nc.vector.tensor_reduce(weight_sum[:, 0], kept[:, 1], AX.X, ALU.add))
                then(nc.vector.tensor_scalar(weight_sum[:, 1], weight_sum[:, 0], 1e-20, None, ALU.add))
                nc.vector.reciprocal(weight_sum[:, 2], weight_sum[:, 1]).then_inc(comb_ready, 1)
                dve.wait_ge(comb_ready, 3 * f + 1)
                for copy in range(2):
                    nc.vector.tensor_tensor(comb[:, :, copy, :], kept[:, 1],
                                            weight_sum[:, 2].unsqueeze(2).to_broadcast([HALF, TILES, EXPERTS]),
                                            ALU.mult).then_inc(comb_ready, 1)

            def h_from(q, b):
                dve.wait_ge(tok_ready, 2 * q + b + 1)
                nc.vector.tensor_tensor(
                    h[:, 2 * b:2 * b + 2, :], bank[TOK[b]][0:HALF, 0:2 * C].rearrange("q (t c) -> q t c", t=2),
                    b_tok[:].to_broadcast([HALF, 2, C]), ALU.add).then_inc(h_ready, 1)

            def xt_stacks(q):
                dve.wait_ge(xt_high_in, 2 * q + 1)
                low_part(xt[:, 1, :], bank[TOK[0]][:, 0:PT], xt[:, 0, :]).then_inc(xt_in, 1)
                dve.wait_ge(xt_high_in, 2 * q + 2)
                stack(xt[:, 2, :], xt_high, bank[TOK[1]][:, 0:PT], LOW_CHI).then_inc(xt_in, 1)

            def step(p, attention, experts, following):
                f = p - 1

                def qk_low(g):
                    dve.wait_ge(qk_high_in, 2 * GROUPS * p + g + 1)
                    value = bank[QK[g % len(QK)]][:, 0:PT]
                    if g < GROUPS:
                        stack(q[:, g, :], q_high[:, g, :], value, LOW_HD).then_inc(qk_in, 1)
                    else:
                        dve.wait_ge(qk_in, 2 * GROUPS * p + g - GROUPS + 1)
                        nc.vector.scalar_tensor_tensor(out=k[:, 1, g - GROUPS, :], in0=value, scalar=k_far[:, 0:1],
                                                       in1=plain(k[:, 0, g - GROUPS, :]), op0=ALU.add,
                                                       op1=ALU.subtract).then_inc(qk_in, 1)

                if experts:
                    for b in range(2):
                        dve.wait_ge(h2_ready, 2 * f + b + 1)
                        statistics(1, h2, b)
                    normalise_begin(1, f)
                if attention:
                    qk_low(0)
                if experts:
                    normalise_end(1, f, h2, xn2)
                if attention:
                    for g in (1, 2):
                        qk_low(g)
                if experts:
                    dve.wait_ge(x2t_high_in, 2 * f + 1)
                    low_part(x2t[:, 1, :], bank[X2T[0]][:, 0:PT], x2t[:, 0, :]).then_inc(x2t_in, 1)
                    dve.wait_ge(x2t_high_in, 2 * f + 2)
                    stack(x2t[:, 2, :], high[:], bank[X2T[1]][:, 0:PT], LOW_CHI).then_inc(x2t_in, 1)
                if attention:
                    for g in range(3, 2 * GROUPS):
                        qk_low(g)
                if experts:
                    route(f)
                if attention:
                    dve.wait_ge(v_raw_in, 2 * p + 1)

                def gated_square(n):
                    count = HT * f + n
                    value = bank[FC][:, 0:PT]
                    dve.wait_ge(fc_ready, count + 1)
                    dve.wait_ge(gate_in, RT * f + n - EARLY + 1)
                    dve.wait_ge(hid_ready, count)
                    nc.vector.scalar_tensor_tensor(out=r[:, n % 2, :], in0=value, scalar=0.0, in1=gate[:],
                                                   op0=ALU.max, op1=ALU.mult).then_inc(gated_ready, 1)
                    dve.wait_ge(gated_ready, (HT - RELUS) * f + n + 1 - relus(n + 1))
                    if n >= HID_BUFS:
                        dve.wait_ge(hid_used, HID_REUSED * f + n - HID_BUFS + 1)
                    nc.vector.tensor_tensor(hid[:, n % HID_BUFS, :], value, r[:, n % 2, :], ALU.mult).then_inc(hid_ready, 1)

                def bias_and_max(u, e):
                    img, hp = divmod(u, HEADS // 2)
                    sc = probs[:, u % 3, e]
                    done = 2 * UNITS * p + 2 * u + e
                    dve.wait_ge(scores_in, done + 1)
                    for i, m in enumerate((2, 1, 0)):
                        for half in range(2):
                            lo, hi = window(half, m)
                            if i:
                                dve.wait_ge(biased, 6 * done + 2 * i + half - 1)
                            at = (2 * hp + e) * NEAR + m
                            nc.vector.scalar_tensor_tensor(
                                out=sc[:, half, lo:hi], in0=masks[:, half, m, lo:hi],
                                scalar=diff[:, 2 * img + half, at:at + 1], in1=sc[:, half, lo:hi],
                                op0=ALU.mult, op1=ALU.add).then_inc(biased, 1)
                    dve.wait_ge(biased, 6 * done + 6)
                    nc.vector.tensor_reduce(neg_max[:, u % 2, e, :], sc, AX.X, ALU.max, negate=True).then_inc(max_ready, 1)

                for s in range(SLOTS):
                    if attention and s == UNITS // 2:
                        dve.wait_ge(v_raw_in, 2 * p + 2)
                    if attention and s < UNITS:
                        bias_and_max(s, 0)
                    if experts and s == 0:
                        dve.wait_ge(comb_high_in, f + 1)
                        stack(comb_t, high[0:2 * EXPERTS, :], bank[GATE][0:2 * EXPERTS, 0:PT], LOW_EXPERT,
                              2 * EXPERTS).then_inc(combt_in, 1)
                    if attention and s < UNITS:
                        bias_and_max(s, 1)
                    if experts and s < RT and by_vector(s + EARLY):
                        gated_square(s + EARLY)
                    if following and s == UNITS:
                        dve.wait_ge(h_pb_ready, p + 1)
                        h_from(p + 1, 0)
                        dve.wait_ge(h_ready, 2 * p + 3)
                        statistics(0, h, 0)
                    if attention and s == UNITS:
                        dve.wait_ge(probs_ready, 2 * UNITS * (p + 1))
                        nc.vector.reciprocal(inv_sum[:, :, 0, :], prob_sum[:]).then_inc(inv_half, 1)
                        dve.wait_ge(inv_half, p + 1)
                        nc.vector.tensor_copy(inv_sum[:, :, 1, :], inv_sum[:, :, 0, :]).then_inc(inv_ready, 1)
                    if following and s == UNITS + 1:
                        h_from(p + 1, 1)
                        dve.wait_ge(h_ready, 2 * p + 4)
                        statistics(0, h, 1)
                        normalise_begin(0, p + 1)
                    if attention and s == UNITS + 1:
                        dve.wait_ge(inv_high_in, p + 1)
                        stack(inv_t, high[0:2 * HEADS, :], bank[SCORE[0]][0:2 * HEADS, 0:PT], LOW_HEAD,
                              2 * HEADS).then_inc(inv_in, 1)

                def o_norm(g):
                    dve.wait_ge(inv_spread, GROUPS * p + g + 1)
                    dve.wait_ge(o_in, OGROUPS * p + GROUPS + g + 1)
                    nc.vector.tensor_tensor(o[:, g, :], bank[SPREAD[g]][:, 0:PT], o[:, g, :], ALU.mult).then_inc(o_normed, 1)

                if attention:
                    for g in range(GROUPS - 1):
                        o_norm(g)
                if following:
                    dve.wait_ge(v_in, 2 * p + 2)
                    normalise_end(0, p + 1, h, xn)
                for b in range(2):
                    if experts:
                        dve.wait_ge(y_ready, 2 * f + b + 1)
                        if b == 0:
                            dve.wait_ge(y_free, 16 * f + 16)
                        nc.vector.tensor_tensor(y[:, 2 * b:2 * b + 2, :],
                                                bank[Y[b]][0:HALF, 0:2 * C].rearrange("q (t c) -> q t c", t=2),
                                                h2[:, 2 * b:2 * b + 2, :], ALU.add).then_inc(y_in, 1)
                    if attention and b == 0:
                        o_norm(GROUPS - 1)
                if following:
                    xt_stacks(p + 1)
                if attention:
                    for b in range(2):
                        dve.wait_ge(proj_ready, 2 * p + b + 1)
                        if experts:
                            dve.wait_ge(y_in, 2 * f + b + 1)
                        dve.wait_ge(h_pb_ready, p + 1)
                        nc.vector.tensor_tensor(h2[:, 2 * b:2 * b + 2, :],
                                                bank[Y[b]][0:HALF, 0:2 * C].rearrange("q (t c) -> q t c", t=2),
                                                h_pb[:, 2 * b:2 * b + 2, :], ALU.add).then_inc(h2_ready, 1)

            h_from(0, 0)
            h_from(0, 1)
            dve.wait_ge(h_ready, 2)
            statistics(0, h, 0)
            statistics(0, h, 1)
            normalise_begin(0, 0)
            normalise_end(0, 0, h, xn)
            xt_stacks(0)
            iterations(dve, step)

        @block.tensor
        def _(pe):
            pe.wait_ge(weights_in, ALL_IN)
            pe.wait_ge(weights_split, 3)
            for c in range(2):
                for kt, kn in ((0, CLO), (1, CHI)):
                    last = nc.tensor.matmul(bank[c][:, 0:HEADS * NEAR], w_qo[0:kn, kt, c * 128:(c + 1) * 128],
                                            rpe_d[0:kn, kt, :], start=kt == 0, stop=kt == 1)
                last.then_inc(bias_w_ready, 1)
            pe.wait_ge(bias_w_in, 3)
            pe.wait_ge(v_padded, 3)

            def transposes(src, banks, ready):
                for c in range(2):
                    for t in range(TILES):
                        last = nc.tensor.transpose(bank[banks[c]][:, t * HALF:(t + 1) * HALF],
                                                   src[:, t, c * 128:(c + 1) * 128], ident[0:HALF, 0:HALF])
                    last.then_inc(ready, 1)

            def channels(out_ap, w, xs, stationary_x):
                terms = ((w(0, 0), xs(0), 128), (w(0, 0), xs(1), 128), (w(1, 0), xs(0), 128),
                         (w(0, 1), xs(2), 128), (w(1, 1), xs(2), CHI))
                for i, (wa, xa, rows) in enumerate(terms):
                    left, right = (xa, wa) if stationary_x else (wa, xa)
                    last = nc.tensor.matmul(out_ap, left[0:rows], right[0:rows], start=i == 0, stop=i == len(terms) - 1)
                return last

            def patch_products(q, t):
                if t == 0:
                    pe.wait_ge(x_in, 16 * q + 16)
                for kt in range(KX):
                    last = nc.tensor.matmul(bank[TOK[t // 2]][0:HALF, (t % 2) * C:(t % 2 + 1) * C],
                                            x[:, kt, t * HALF:(t + 1) * HALF], w_tok[:, kt, :],
                                            start=kt == 0, stop=kt == KX - 1)
                if t % 2 == 1:
                    last.then_inc(tok_ready, 1)

            def x_transposed(q):
                pe.wait_ge(xn_ready[0], q + 1)
                transposes(xn, TOK, xt_ready)

            def step(p, attention, experts, following):
                f = p - 1
                if attention:
                    pe.wait_ge(xt_in, 2 * p + 2)
                    for g in range(2 * GROUPS):
                        channels(bank[QK[g % len(QK)]][:, 0:PT], lambda part, c: w_qk[:, part, c, g * 128:(g + 1) * 128],
                                 lambda i: xt[:, i, :], False).then_inc(qk_ready, 1)

                def v_product(b):
                    for t in (2 * b, 2 * b + 1):
                        last = channels(bank[V[b]][0:HALF, (t % 2) * VD:(t % 2 + 1) * VD],
                                        lambda part, c: w_vd[:, part, c], lambda i: xt[:, i, t * HALF:(t + 1) * HALF],
                                        True)
                    last.then_inc(v_ready, 1)

                if attention:
                    if experts:
                        pe.wait_ge(h2_ready, 2 * p)
                    v_product(0)
                if experts:
                    pe.wait_ge(xn_ready[1], f + 1)
                    if attention:
                        pe.wait_ge(qk_in, 2 * GROUPS * p + 2)
                    transposes(xn2, X2T, x2t_ready)
                if experts:
                    pe.wait_ge(x2t_in, 2 * f + 2)

                def hidden(n):
                    j, rows = HIDDEN_ORDER[n], rows_of(HIDDEN_ORDER[n])
                    if n >= EARLY and by_vector(n - 1):
                        pe.wait_ge(hid_ready, HT * f + n)
                    elif n >= EARLY:
                        pe.wait_ge(r_ready, RELUS * f + relus(n))
                    elif attention:
                        pe.wait_ge(qk_in, 2 * GROUPS * p + len(TOK) + n + 1)
                    else:
                        pe.wait_ge(r_ready, RELUS * f)
                        pe.wait_ge(gate_in, RT * f)
                    if n == 0:
                        rows += EXPERTS
                    channels(fc_bank(n)[0:rows, 0:PT], lambda part, c: w_fc[:, part, c, j * 128:j * 128 + rows],
                             lambda i: x2t[:, i, :], False).then_inc(fc_ready, 1)

                if experts:
                    for n in range(EARLY):
                        hidden(n)
                    pe.wait_ge(logits_in, f + 1)
                    for t in range(TILES):
                        last = nc.tensor.matmul(bank[X2T[0]][0:HALF, t * EXPERTS:(t + 1) * EXPERTS],
                                                logits_t[:, t * HALF:(t + 1) * HALF],
                                                ident[LAST_ROWS:LAST_ROWS + EXPERTS, LAST_ROWS:LAST_ROWS + EXPERTS],
                                                start=True, stop=True)
                    last.then_inc(logits_ready, 1)
                if attention:
                    pe.wait_ge(qk_in, 2 * GROUPS * (p + 1))

                def scores(u, e):
                    img, hp = divmod(u, HEADS // 2)
                    if u:
                        pe.wait_ge(scores_in, 2 * UNITS * p + 2 * u + e - 1)
                    g, slot = divmod(2 * hp + e, 4)
                    high = slice(slot * SLOT, slot * SLOT + HD)
                    both = slice(slot * SLOT, (slot + 1) * SLOT)
                    keys = slice(img * TOKENS, (img + 1) * TOKENS)
                    for half in range(2):
                        at = bank[SCORE[e]][0:HALF, half * TOKENS:(half + 1) * TOKENS]
                        queries = slice(img * TOKENS + half * HALF, img * TOKENS + (half + 1) * HALF)
                        nc.tensor.matmul(at, q[both, g, queries], k[both, 0, g, keys], start=True, stop=False)
                        last = nc.tensor.matmul(at, q[high, g, queries], k[high, 1, g, keys], start=False, stop=True)
                    last.then_inc(scores_ready, 1)

                def gates(i):
                    pe.wait_ge(combt_in, f + 1)
                    if i:
                        pe.wait_ge(gate_in, RT * f + i)
                    nc.tensor.matmul(bank[GATE][:, 0:PT], expert_sel[:, i, :], comb_t, start=True,
                                     stop=True).then_inc(gate_ready, 1)

                def probs_transposed(u, jt):
                    if jt == 0:
                        pe.wait_ge(probs_ready, 2 * UNITS * p + 2 * u + 2)
                    if u or jt:
                        pe.wait_ge(probst_in, 2 * UNITS * p + 2 * u + jt)
                    elif experts:
                        pe.wait_ge(exp_ready, f + 1)
                    for e in range(2):
                        for half in range(2):
                            first = e * TOKENS + half * HALF
                            last = nc.tensor.transpose(bank[PROBT][0:HALF, first:first + HALF],
                                                       probs[:, u % 3, e, half, jt * HALF:(jt + 1) * HALF],
                                                       ident[0:HALF, 0:HALF])
                    last.then_inc(probst_ready, 1)

                def values(u):
                    img, hp = divmod(u, HEADS // 2)
                    n = img * GROUPS + hp // 2
                    pe.wait_ge(probs_low_ready, 2 * UNITS * p + 2 * u + 2)
                    if u == 0:
                        pe.wait_ge(v_in, 2 * p + 2)
                    if hp % 2 == 0 and n:
                        pe.wait_ge(o_in, OGROUPS * p + n)
                    terms = [(e, jt, part) for e in range(2) for jt in range(2) for part in (probs_th, probs_tl)]
                    for i, (e, jt, part) in enumerate(terms):
                        last = nc.tensor.matmul(bank[OUT][:, 0:TOKENS], v[:, 2 * img + jt, 2 * hp + e, :],
                                                part[:, u % 2, jt, e * TOKENS:(e + 1) * TOKENS],
                                                start=hp % 2 == 0 and i == 0, stop=hp % 2 == 1 and i == len(terms) - 1)
                    last.then_inc(pv_done, 1)

                def second_product(n, b):
                    j, rows = HIDDEN_ORDER[n], rows_of(HIDDEN_ORDER[n])
                    if b == 0:
                        pe.wait_ge(hid_ready, HT * f + n + 1)
                        if attention and n == 0:
                            pe.wait_ge(v_high_in, 2 * p + 1)
                    if n == 0:
                        nc.tensor.matmul(bank[Y[b]][0:HALF, 0:2 * C], nothing[:, 0:HALF], nothing, start=True, stop=False)
                    for t in (2 * b, 2 * b + 1):
                        last = nc.tensor.matmul(bank[Y[b]][0:HALF, (t % 2) * C:(t % 2 + 1) * C],
                                                hid[0:rows, n % HID_BUFS, t * HALF:(t + 1) * HALF], w_out[0:rows, j, :],
                                                start=False, stop=n == HT - 1 and t % 2 == 1)
                    if n == HT - 1:
                        last.then_inc(y_ready, 1)
                    elif b == 1 and n < HID_REUSED:
                        last.then_inc(hid_used, 1)

                if attention:
                    scores(0, 0)
                    scores(0, 1)
                for s in range(SLOTS):
                    if following and s == UNITS:
                        if experts:
                            pe.wait_ge(r_ready, RELUS * (f + 1))
                            pe.wait_ge(gate_in, RT * (f + 1))
                        patch_products(p + 1, 0)
                        patch_products(p + 1, 1)
                    if following and s == UNITS + 1:
                        patch_products(p + 1, 3)
                    if attention and PROBT_LAG <= s <= UNITS:
                        probs_transposed(s - PROBT_LAG, 0)
                    if experts and 1 < s < RT:
                        gates(s)
                    if attention and s >= VALUE_LAG:
                        values(s - VALUE_LAG)
                    if attention and s == UNITS + 1:
                        probs_transposed(s - PROBT_LAG, 0)
                    if experts and s < RT:
                        hidden(s + EARLY)
                    if experts and s == 1:
                        gates(s)
                    if experts and (s == 0 or EARLY <= s < RT):
                        second_product(s, 0)
                    if following and s == UNITS:
                        patch_products(p + 1, 2)
                    if attention and 0 <= s - PROBT_LAG < UNITS:
                        probs_transposed(s - PROBT_LAG, 1)
                    if attention and s == 1:
                        v_product(1)
                    if attention and s + 1 < UNITS:
                        scores(s + 1, 0)
                        scores(s + 1, 1)
                    if experts and (s == 0 or EARLY <= s < RT):
                        second_product(s, 1)
                    if experts and s == 0:
                        pe.wait_ge(comb_ready, 3 * f + 3)
                        pe.wait_ge(r_ready, RELUS * f + EARLY)
                        for t in range(TILES):
                            last = nc.tensor.transpose(bank[GATE][0:2 * EXPERTS, t * HALF:(t + 1) * HALF],
                                                       comb[:, t].rearrange("q a e -> q (a e)"), ident[0:HALF, 0:HALF])
                        last.then_inc(combt_ready, 1)
                        for n in range(1, EARLY):
                            second_product(n, 0)
                            second_product(n, 1)
                        gates(0)
                    if attention and s == UNITS + 1:
                        pe.wait_ge(inv_ready, p + 1)
                        pe.wait_ge(scores_in, 2 * UNITS * (p + 1))
                        for t in range(TILES):
                            last = nc.tensor.transpose(bank[SCORE[0]][0:2 * HEADS, t * HALF:(t + 1) * HALF],
                                                       inv_sum[:, t].rearrange("q a e -> q (a e)"), ident[0:HALF, 0:HALF])
                        last.then_inc(invt_ready, 1)
                    if experts and RT <= s - 2 < HT:
                        second_product(s - 2, 0)
                        second_product(s - 2, 1)
                    if attention and s == UNITS + 2:
                        pe.wait_ge(inv_in, p + 1)
                        pe.wait_ge(probst_in, 2 * UNITS * (p + 1))
                        for g in range(GROUPS):
                            nc.tensor.matmul(bank[SPREAD[g]][:, 0:PT], head_sel[:, g, :], inv_t, start=True,
                                             stop=True).then_inc(inv_spread, 1)
                if following:
                    x_transposed(p + 1)
                if attention:
                    pe.wait_ge(o_normed, GROUPS * (p + 1))
                    for b in range(2):
                        if experts:
                            pe.wait_ge(y_in, 2 * f + b + 1)
                        for t in (2 * b, 2 * b + 1):
                            for g in range(GROUPS):
                                last = nc.tensor.matmul(bank[Y[b]][0:HALF, (t % 2) * C:(t % 2 + 1) * C],
                                                        o[:, g, t * HALF:(t + 1) * HALF], w_proj[:, g, :],
                                                        start=g == 0, stop=g == GROUPS - 1)
                        last.then_inc(proj_ready, 1)

            for t in range(TILES):
                patch_products(0, t)
            x_transposed(0)
            iterations(pe, step)


def lay_out(i):
    f = np.float32

    def two(w):
        return np.ascontiguousarray(np.stack([w[:CLO], np.concatenate([w[CLO:], w[CLO:]])], 1))

    r = {}
    x = i["x"].reshape(PAIRS, 2, CHANNELS, GRID, PATCH, GRID, PATCH).transpose(0, 2, 4, 6, 1, 3, 5)
    r["x"] = np.ascontiguousarray(x.reshape(PAIRS, KX, 128, PT).transpose(0, 2, 1, 3))
    r["w_tok"] = np.ascontiguousarray(i["L0_tok_W"].T.reshape(KX, 128, C).transpose(1, 0, 2))
    r["b_tok"] = np.ascontiguousarray(np.broadcast_to(i["L0_tok_b"], (HALF, 1, C)))
    w = i["L0_attn_qkv_w"]
    qk = w[:2 * C].T.reshape(C, 2 * GROUPS, 4, HD)
    r["w_qk"] = two(np.concatenate([qk, qk], -1).reshape(C, -1)).reshape(128, -1)
    r["w_qo"] = two(np.concatenate([w[:C], w[:C, CLO:]], 1))
    r["w_v"] = two(np.ascontiguousarray(w[2 * C:].T))
    rpe = i["L0_attn_rpe_w"]
    near, far = np.zeros((HEADS, HD, HEADS, NEAR), f), np.zeros((HEADS, HD, HEADS, NEAR), f)
    k_far = np.ascontiguousarray(np.broadcast_to(rpe[:, NEAR], (4, 2, HD)))
    for n in range(HEADS):
        near[n, :, n, :] = rpe[:, :NEAR]
        far[n, :, n, :] = rpe[:, NEAR:NEAR + 1]
    r["rpe_m"], r["rpe_f"] = two(near.reshape(C, -1)), two(far.reshape(C, -1))
    r["k_far"] = k_far.reshape(128, 1)
    proj = np.zeros((GROUPS, 4, SLOT, C), f)
    proj[:, :, :HD] = proj[:, :, HD:] = i["L0_attn_proj_w"].T.reshape(GROUPS, 4, HD, C)
    r["w_proj"] = np.ascontiguousarray(proj.reshape(GROUPS, 128, C).transpose(1, 0, 2))
    r["b_proj"] = np.ascontiguousarray(np.broadcast_to(i["L0_attn_proj_b"], (HALF, 1, C)))
    fc = np.zeros((C, HT * 128), f)
    fc[:, :EXPERTS * C] = i["L0_ffn_w1"].transpose(1, 0, 2).reshape(C, EXPERTS * C)
    fc[:, EXPERTS * C:HID] = i["L0_ffn_w_fc_sh"]
    fc[:, HID:HID + EXPERTS] = i["L0_ffn_router_w"].T
    r["w_fc"] = two(fc).reshape(128, -1)
    wo = np.zeros((HT * 128, C), f)
    wo[:EXPERTS * C] = i["L0_ffn_w2"].reshape(EXPERTS * C, C)
    wo[EXPERTS * C:HID] = i["L0_ffn_w_proj_sh"]
    r["w_out"] = np.ascontiguousarray(wo.reshape(HT, 128, C).transpose(1, 0, 2))
    r["b_rt"] = np.ascontiguousarray(np.broadcast_to(i["L0_ffn_balance_bias"], (HALF, TILES, EXPERTS)))
    b = buckets().reshape(2, HALF, TOKENS)
    r["masks"] = np.ascontiguousarray(np.stack([b == m for m in range(NEAR)], 2).transpose(1, 0, 2, 3).reshape(HALF, 2, -1).astype(f))
    r["ident"] = np.eye(128, dtype=f)
    twice = lambda n: np.tile(np.arange(n), 2)[:, None]
    r["selectors"] = np.zeros((SLOT + 2 * HEADS, RT * 128), f)
    r["selectors"][:2 * EXPERTS] = twice(EXPERTS) == np.arange(RT * 128) // C
    r["selectors"][SLOT:, :GROUPS * 128] = twice(HEADS) == np.arange(GROUPS * 128) // SLOT
    row = np.arange(128)
    low = [row >= CHI, row % SLOT >= HD, row >= EXPERTS, row >= HEADS]
    r["low_rows"] = np.where(np.stack(low, 1), -1.0, 0.0).astype(f)
    r["expert_no"] = np.ascontiguousarray(np.broadcast_to(np.arange(EXPERTS, dtype=f), (HALF, TILES, EXPERTS)))
    return r


def kernel(**inputs):
    import concourse.bacc as bacc
    from concourse.bass_utils import run_bass_kernel_spmd

    arrays = lay_out({k: np.asarray(v) for k, v in inputs.items()})
    nc = bacc.Bacc("TRN2", target_bir_lowering=False, num_devices=1)
    args = {k: nc.dram_tensor(f"in_{k}", v.shape, mybir.dt.from_np(v.dtype), kind="ExternalInput").ap()
            for k, v in arrays.items()}
    out = nc.dram_tensor("out", (PAIRS, TILES, HALF, C), mybir.dt.float32, kind="ExternalOutput").ap()
    vit_kernel(nc, args, out)
    got = run_bass_kernel_spmd(nc, [{f"in_{k}": v for k, v in arrays.items()}], core_ids=[0])
    return got.results[0]["out"].reshape(IMAGES, TOKENS, C)
```
